# Optimizing a Trainium2 kernel written in Bass

```python
import numpy as np
import jax
import jax.numpy as jnp

def _softmax(x, axis=-1):
    return jax.nn.softmax(x, axis=axis)

def _gelu(x):
    return jax.nn.gelu(x, approximate=True)

def _silu(x):
    return jax.nn.silu(x)

def _sigmoid(x):
    return jax.nn.sigmoid(x)

def _layernorm(x, axis=-1, eps=1e-05):
    m = jnp.mean(x, axis=axis, keepdims=True)
    v = jnp.var(x, axis=axis, keepdims=True)
    return (x - m) / jnp.sqrt(v + eps)

def _scatter_add(tgt, idx, src, axis=0):
    return tgt.at[idx].add(src)

def _segment_sum(src, seg, n):
    return jax.ops.segment_sum(src, seg, n)
kernel_name = 'mk_decoder_preln_d1_seqx_r4_3567b8'

def setup_inputs(seed: int=0):
    np.random.seed(seed)
    _w = jnp.asarray

    def _rec_inputs():
        import jax
        import jax.numpy as jnp
        _rk = jax.random.key(seed)
        x = 7.22e-05 + 1 * jax.random.normal(jax.random.fold_in(_rk, 1), (64, 256, 256), jnp.float32)
        _lenS = 256 - jax.random.randint(jax.random.fold_in(_rk, 7), (64,), 0, max(1, 256 // 4) + 1, jnp.int32)
        _lenS2 = 120 - jax.random.randint(jax.random.fold_in(_rk, 8), (64,), 0, max(1, 120 // 4) + 1, jnp.int32)
        _ctx_1024P = jax.random.normal(jax.random.fold_in(_rk, 11), (64, 16, 256), jnp.float32)
        _ctx_1024c = jax.random.dirichlet(jax.random.fold_in(_rk, 511), 0.3 * jnp.ones((16,), jnp.float32), (64, 120))
        _ctx_1024t = jnp.einsum('bsk,bkd->bsd', _ctx_1024c, _ctx_1024P)
        _ctx_1024t = _ctx_1024t * jax.lax.rsqrt(jnp.mean(jnp.square(_ctx_1024t)) + 1e-12) * 0.953939
        ctx_1024 = 4.13588e-05 + 0.999923 * (_ctx_1024t + 0.3 * jax.random.normal(jax.random.fold_in(_rk, 611), (64, 120, 256), jnp.float32))
        return (x, ctx_1024)
    x, ctx_1024 = _rec_inputs()

    def _L0_attn_setup():
        import jax, jax.numpy as jnp
        import numpy as np
        import math
        N_EMBD = 256
        N_HEAD = 16
        N_LAYER = 12
        key = jax.random.key(seed)
        kx, kw, kb = jax.random.split(key, 3)
        B, T, C = (4, 512, N_EMBD)
        x = jax.random.normal(kx, (B, T, C), dtype=jnp.float32)
        bound = 1.0 / math.sqrt(C)
        W = jax.random.uniform(kw, (3 * C, C), minval=-bound, maxval=bound, dtype=jnp.float32)
        W = W * (1.0 / math.sqrt(N_LAYER * 2))
        b = jax.random.uniform(kb, (3 * C,), minval=-bound, maxval=bound, dtype=jnp.float32)
        return {'x': x, 'W': W, 'b': b}
    _L0_attn_all = _L0_attn_setup()
    _L0_attn_in = {k: v for k, v in _L0_attn_all.items() if k in ('W', 'b')}
    del _L0_attn_all

    def _L0_xattn_setup():
        import jax, jax.numpy as jnp
        import numpy as np
        N_HEAD = 16
        key = jax.random.key(seed)
        ks = jax.random.split(key, 5)
        b, l, d = (4, 512, 256)
        dh = d // N_HEAD
        return {'q': jax.random.normal(ks[0], (b, l, d), dtype=jnp.float32), 'kv': jax.random.normal(ks[1], (b, l, d), dtype=jnp.float32), 'Wq': jax.random.normal(ks[2], (d, d), dtype=jnp.float32) * 0.02, 'Wkv': jax.random.normal(ks[3], (2 * dh, d), dtype=jnp.float32) * 0.02, 'Wc': jax.random.normal(ks[4], (d, d), dtype=jnp.float32) * 0.02}
    _L0_xattn_all = _L0_xattn_setup()
    _L0_xattn_in = {k: v for k, v in _L0_xattn_all.items() if k in ('Wq', 'Wkv', 'Wc')}
    del _L0_xattn_all

    def _L0_ffn_setup():
        import jax, jax.numpy as jnp
        import numpy as np
        H = 256
        I = 1024
        E = 4
        LN_EPS = 1e-12

        def _layer_norm(x, gamma, beta, eps=LN_EPS):
            mu = jnp.mean(x, axis=-1, keepdims=True)
            var = jnp.mean(jnp.square(x - mu), axis=-1, keepdims=True)
            return (x - mu) * jax.lax.rsqrt(var + eps) * gamma + beta
        key = jax.random.key(seed)
        ks = jax.random.split(key, 8)
        B, S = (4, 128)
        scale = 0.02
        return {'hidden_states': jax.random.normal(ks[0], (B, S, H), jnp.float32), 'W_router': jax.random.normal(ks[1], (H, E), jnp.float32) * scale, 'W1': jax.random.normal(ks[2], (E, H, I), jnp.float32) * scale, 'b1': jax.random.normal(ks[3], (E, I), jnp.float32) * scale, 'Wo': jax.random.normal(ks[4], (I, H), jnp.float32) * scale, 'bo': jax.random.normal(ks[5], (H,), jnp.float32) * scale, 'ln_gamma': jnp.ones((H,), jnp.float32), 'ln_beta': jnp.zeros((H,), jnp.float32)}
    _L0_ffn_all = _L0_ffn_setup()
    _L0_ffn_in = {k: v for k, v in _L0_ffn_all.items() if k in ('W_router', 'W1', 'b1', 'Wo', 'bo', 'ln_gamma', 'ln_beta')}
    del _L0_ffn_all
    return {'x': x, 'ctx_1024': ctx_1024, 'L0_attn_W': _L0_attn_in['W'], 'L0_attn_b': _L0_attn_in['b'], 'L0_xattn_Wq': _L0_xattn_in['Wq'], 'L0_xattn_Wkv': _L0_xattn_in['Wkv'], 'L0_xattn_Wc': _L0_xattn_in['Wc'], 'L0_ffn_W_router': _L0_ffn_in['W_router'], 'L0_ffn_W1': _L0_ffn_in['W1'], 'L0_ffn_b1': _L0_ffn_in['b1'], 'L0_ffn_Wo': _L0_ffn_in['Wo'], 'L0_ffn_bo': _L0_ffn_in['bo'], 'L0_ffn_ln_gamma': _L0_ffn_in['ln_gamma'], 'L0_ffn_ln_beta': _L0_ffn_in['ln_beta']}

def reference(x, ctx_1024, L0_attn_W, L0_attn_b, L0_xattn_Wq, L0_xattn_Wkv, L0_xattn_Wc, L0_ffn_W_router, L0_ffn_W1, L0_ffn_b1, L0_ffn_Wo, L0_ffn_bo, L0_ffn_ln_gamma, L0_ffn_ln_beta):
    import jax
    import jax.numpy as jnp

    def _L0_attn_ref(x, W, b):
        import jax, jax.numpy as jnp
        import numpy as np
        import math
        N_EMBD = 256
        N_HEAD = 16
        N_LAYER = 12
        B, T, C = x.shape
        H = N_HEAD
        D = C // H
        qkv = jnp.einsum('btc,oc->bto', x, W) + b
        q, k, v = jnp.split(qkv, 3, axis=-1)
        q = q.reshape(B, T, H, D).transpose(0, 2, 1, 3)
        k = k.reshape(B, T, H, D).transpose(0, 2, 1, 3)
        v = v.reshape(B, T, H, D).transpose(0, 2, 1, 3)
        att = jnp.einsum('bhtd,bhsd->bhts', q, k) / math.sqrt(D)
        causal = jnp.tril(jnp.ones((T, T), dtype=bool))
        att = jnp.where(causal, att, -jnp.inf)
        att = jax.nn.softmax(att, axis=-1)
        y = jnp.einsum('bhts,bhsd->bhtd', att, v)
        return y.transpose(0, 2, 1, 3).reshape(B, T, C)

    def _L0_xattn_ref(q, kv, Wq, Wkv, Wc):
        import jax, jax.numpy as jnp
        import numpy as np
        N_HEAD = 16
        b, l, d = q.shape
        h = N_HEAD
        dh = d // h
        qp = jnp.einsum('bld,ed->ble', q, Wq)
        scores = jnp.einsum('bld,bmd->blm', qp, kv)
        idx = jnp.argmax(scores, axis=-1)
        mem = jnp.take_along_axis(kv, idx[..., None], axis=1)
        mkv = jnp.einsum('bld,ed->ble', mem, Wkv)
        mk, mv = jnp.split(mkv, 2, axis=-1)
        qh = qp.reshape(b, l, h, dh).transpose(0, 2, 1, 3)
        scale = 1.0 / np.sqrt(dh).astype(np.float32)
        logits = jnp.einsum('bhld,bmd->bhlm', qh, mk) * scale
        attn = jax.nn.softmax(logits, axis=-1)
        out = jnp.einsum('bhlm,bmd->bhld', attn, mv)
        out = out.transpose(0, 2, 1, 3).reshape(b, l, d)
        return jnp.einsum('bld,ed->ble', out, Wc)

    def _L0_ffn_ref(hidden_states, W_router, W1, b1, Wo, bo, ln_gamma, ln_beta):
        import jax, jax.numpy as jnp
        import numpy as np
        H = 256
        I = 1024
        E = 4
        LN_EPS = 1e-12

        def _layer_norm(x, gamma, beta, eps=LN_EPS):
            mu = jnp.mean(x, axis=-1, keepdims=True)
            var = jnp.mean(jnp.square(x - mu), axis=-1, keepdims=True)
            return (x - mu) * jax.lax.rsqrt(var + eps) * gamma + beta
        B, S, _ = hidden_states.shape
        x = hidden_states.reshape(-1, H)
        logits = x @ W_router
        expert_idx = jnp.argmax(logits, axis=-1)
        h = jnp.einsum('th,ehi->tei', x, W1) + b1
        h = jax.nn.gelu(h, approximate=False)
        onehot = jax.nn.one_hot(expert_idx, E, dtype=x.dtype)
        intermediate = jnp.einsum('te,tei->ti', onehot, h)
        y = intermediate @ Wo + bo + x
        y = _layer_norm(y, ln_gamma, ln_beta)
        return y.reshape(B, S, H)
    x = x + _L0_attn_ref(_layernorm(x, axis=-1), L0_attn_W, L0_attn_b)
    x = x + _L0_xattn_ref(_layernorm(x, axis=-1), ctx_1024, L0_xattn_Wq, L0_xattn_Wkv, L0_xattn_Wc)
    x = x + _L0_ffn_ref(_layernorm(x, axis=-1), L0_ffn_W_router, L0_ffn_W1, L0_ffn_b1, L0_ffn_Wo, L0_ffn_bo, L0_ffn_ln_gamma, L0_ffn_ln_beta)
    return x

_drawn_inputs = setup_inputs


def setup_inputs(seed=0):
    import zlib

    import numpy as np

    out = dict(_drawn_inputs(seed))
    spreads = {'L0_ffn_ln_gamma': (1.0, 0.2), 'L0_ffn_ln_beta': (0.0, 0.1)}
    factors = {'L0_attn_W': 2.939, 'L0_xattn_Wq': 5.263, 'L0_ffn_b1': 8.0, 'L0_ffn_bo': 5.401}
    for name, (base, spread) in spreads.items():
        noise = np.random.default_rng([zlib.crc32(name.encode()), seed]).standard_normal(out[name].shape)
        drawn = base * np.exp(spread * noise) if base else spread * noise
        out[name] = jnp.asarray(drawn.astype(out[name].dtype))
    for name, factor in factors.items():
        out[name] = (out[name] * factor).astype(out[name].dtype)
    return out
```

```python
from contextlib import ExitStack

import concourse.bass as bass
from concourse import mybir
from concourse.alu_op_type import AluOpType as ALU

F32 = mybir.dt.float32
BF16 = mybir.dt.bfloat16
U32 = mybir.dt.uint32
I32 = mybir.dt.int32
ACT = mybir.ActivationFunctionType
AX_X = mybir.AxisListType.X

P = 128
C = 256
KC = C // P
T = 256
NT = T // P
H = 16
D = C // H
HP = H // KC
M = 120
E = 4
I = 1024
NTERM = 6
KR = NTERM * D
NEG = -1e30
LN_EPS = 1e-5
LAGS = 4
TILE = 512
TS = TILE // P
MI = I // P
ROW = C + 1
OUT_LN_EPS = 1e-12
Q_PARTS = (0, 0, 0, 1, 1, 2)
K_PARTS = (0, 1, 2, 0, 1, 0)


BEFORE = 3 * P + M + 3 + E
NEXT_ROW = BEFORE + P
NUMBERS = NEXT_ROW + E
TILE_NOS = NUMBERS + 2 * NT


class Signal:

    def __init__(self, sem, per_sequence):
        self.sem = sem
        self.per_sequence = per_sequence

    def value(self, b, k=None):
        return b * self.per_sequence + (self.per_sequence if k is None else k)


def begun(b):
    return not isinstance(b, int) or b >= 0


def decoder_kernel(nc, x, ctxT, wqkvT, bqkT, bv, wqT, wkvT, wcT, w_router, w1, b1T, wo, bo, gamma, beta, consts, out):
    B = x.shape[0]
    assert B % 2 == 0 and B >= 8

    with ExitStack() as stack:
        def sb(name, shape, dt=F32):
            return stack.enter_context(nc.sbuf_tensor(name, shape, dt))

        def signal(name, per_sequence, step=1):
            return Signal(stack.enter_context(nc.semaphore(name)), per_sequence * step)

        def dma_signal(name, per_sequence):
            return [Signal(stack.enter_context(nc.semaphore(f"{name}{par}")), 16 * per_sequence) for par in range(2)]

        def semaphore(name):
            return stack.enter_context(nc.semaphore(name))

        psum = stack.enter_context(nc.psum_tensor("psum", [P, 8, 512], F32))
        S_BANKS, ST_BANKS, Y_BANKS, MISC_BANKS = (0, 1), (2, 3), (4, 5), (6, 7)

        parts_dram = {
            name: nc.dram_tensor(f"parts_{name}", (2, 3, HP, D, KC * T), BF16).ap() for name in ("q", "k", "qc")
        }

        ROOM = B * T + TILE
        rows_dram = nc.dram_tensor("rows_dram", (E * ROOM + TILE, ROW), F32).ap()

        ident_bf = sb("ident_bf", [P, P], BF16)
        ones_bf = sb("ones_bf", [P, P], BF16)
        mask_s = sb("mask_s", [P, P], BF16)
        mask_t = sb("mask_t", [P, P], BF16)
        consts_sb = sb("consts_sb", [P, TILE_NOS + B * T // TILE + E - 1])
        iota_m = consts_sb[:, 3 * P:3 * P + M]
        part_mask = consts_sb[:, 3 * P + M:3 * P + M + 3]
        ident = consts_sb[:, 0:P]
        minus_half = sb("minus_half", [P, TS])
        wqkv_sb = sb("wqkv_sb", [P, KC, 3 * C])
        bqk_sb = sb("bqk_sb", [P, 2 * KC])
        bv_sb = sb("bv_sb", [P, C])
        wq_sb = sb("wq_sb", [P, KC, C])
        wmk_sb = sb("wmk_sb", [P, KC, KR])
        wmv_sb = sb("wmv_sb", [P, KC, D])
        wc_sb = sb("wc_sb", [P, KC, C])

        x_in = sb("x_in", [P, 2, NT, C])
        x_res = sb("x_res", [P, 2, NT, C])
        ctx_sb = sb("ctx_sb", [P, 2, KC, M])
        stats = sb("stats", [P, NT, 6])
        mv = sb("mv", [P, NT, 2])
        rstd = sb("rstd", [P, NT])
        z = sb("z", [P, NT, C])
        zT = sb("zT", [P, KC, T])
        q_parts = sb("q_parts", [P, 3, KC * T], BF16)
        q_rest = sb("q_rest", [P, KC * T])
        k_parts = sb("k_parts", [P, 3, KC * T], BF16)
        k_rest = sb("k_rest", [P, KC * T])
        QP = sb("QP", [P, 2, H, T], BF16)
        KP = sb("KP", [P, 2, H, T], BF16)
        V = sb("V", [P, 2, NT, H, 2 * D])
        negmax = sb("negmax", [P, NT, H])
        mx2 = sb("mx2", [P, NT, 2, H], BF16)
        mxT = sb("mxT", [2 * H, T], BF16)
        PA = sb("PA", [P, H, T])
        PB = sb("PB", [P, H, P])
        yT = sb("yT", [P, H // 4, T])
        rsum = sb("rsum", [P, NT, H])
        y = sb("y", [P, NT, C])
        x1 = sb("x1", [P, 2, NT, C])
        cz = sb("cz", [P, NT, C])
        czT = sb("czT", [P, KC, T])
        cstats = sb("cstats", [P, NT, 6])
        cmv = sb("cmv", [P, NT, 2])
        crstd = sb("crstd", [P, NT])
        cqT = sb("cqT", [P, KC * T])
        cq_parts = sb("cq_parts", [P, 3, KC * T], BF16)
        cq_rest = sb("cq_rest", [P, KC * T])
        QC = sb("QC", [P, 2, H, T], BF16)
        KCx = sb("KCx", [P, 2, P], BF16)
        kc32 = sb("kc32", [P, M])
        kc_h = sb("kc_h", [P, M], BF16)
        kc_m = sb("kc_m", [P, M], BF16)
        kc_r = sb("kc_r", [P, M])
        kc_r2 = sb("kc_r2", [P, M])
        kc_a = sb("kc_a", [P, M])
        kc_b = sb("kc_b", [P, M])
        cv = sb("cv", [P, D])
        VC = sb("VC", [P, 2, 2 * D])
        cnt_sb = sb("cnt_sb", [P, 1])
        top8 = sb("top8", [P, NT, 8])
        top8i = sb("top8i", [P, NT, 8], U32)
        first = sb("first", [P, NT])
        onehot = sb("onehot", [P, NT, M], BF16)
        cnegmax = sb("cnegmax", [P, NT, H])
        cmx2 = sb("cmx2", [P, NT, 2, H], BF16)
        cmxT = sb("cmxT", [2 * H, T], BF16)
        PC = sb("PC", [P, H, T])
        cyT = sb("cyT", [P, H // 4, T])
        crsum = sb("crsum", [P, NT, H])
        cy = sb("cy", [P, NT, C])
        cyC = sb("cyC", [P, KC, T])
        x2 = sb("x2", [P, 2, NT, ROW])
        rz = sb("rz", [P, NT, C])
        rzT = sb("rzT", [P, KC, T])
        rstats = sb("rstats", [P, NT, 6])
        rmv = sb("rmv", [P, NT, 2])
        rrstd = sb("rrstd", [P, NT])
        wr_sb = sb("wr_sb", [P, KC, E])
        before_bf = sb("before_bf", [P, P], BF16)
        prefer = consts_sb[:, 3 * P + M + 3:3 * P + M + 3 + E]
        greatest = sb("greatest", [P, NT])
        equal = sb("equal", [P, NT, E])
        chosen = sb("chosen", [P, NT, E])
        chosen_bf = sb("chosen_bf", [P, NT, E], BF16)
        place = sb("place", [P, NT, E])
        row_no = sb("row_no", [P, NT])
        row_u = sb("row_u", [P, 2, NT], U32)
        next_row = sb("next_row", [P, E])

        TILES = B * T // TILE + E - 1
        w1_sb = QP[:].bitcast(F32).rearrange("p s h n -> p (s h n)").rearrange("p (s c i) -> p s c i", s=2, c=KC)
        kp_space = KP[:].bitcast(F32).rearrange("p s h n -> p (s h n)").rearrange("p (s j c) -> p s j c", j=TS, c=C)
        zb = kp_space[:, 0:2]
        xb = kp_space[:, 2:4]
        qc_space = QC[:].bitcast(F32).rearrange("p s h n -> p (s h n)").rearrange("p (s j c) -> p s j c", j=TS, c=C)
        fz = qc_space[:, 0]
        ysum = qc_space[:, 1]
        fzT = qc_space[:, 2].rearrange("p j c -> p (j c)").rearrange("p (c n) -> p c n", c=KC)
        hT = PA[:].rearrange("p h n -> p (h n)").rearrange("p (m n) -> p m n", m=MI)
        final = PB[:].rearrange("p h n -> p (h n)").rearrange("p (s j c) -> p s j c", s=2, j=TS)
        b1_sb = sb("b1_sb", [P, 2, MI])
        wo_sb = sb("wo_sb", [P, MI, C])
        bo_sb = sb("bo_sb", [P, C])
        gamma_sb = sb("gamma_sb", [P, C])
        beta_sb = sb("beta_sb", [P, C])
        padding = sb("padding", [P, TS, ROW])
        count_f = sb("count_f", [P, E])
        count_i = sb("count_i", [P, E], I32)
        tiles_f = sb("tiles_f", [P, E])
        jump = sb("jump", [P, E])
        past = sb("past", [P, E, TILES])
        tile_row = sb("tile_row", [P, TILES])
        tile_expert = sb("tile_expert", [P, TILES])
        next_u = sb("next_u", [P, E], U32)
        tile_row_u = sb("tile_row_u", [P, TILES], U32)
        tile_expert_u = sb("tile_expert_u", [P, TILES], U32)
        fx = sb("fx", [P, 2, TS, ROW])
        fstats = sb("fstats", [P, TS, 6])
        fmv = sb("fmv", [P, TS, 2])
        frstd = sb("frstd", [P, TS])
        ostats = sb("ostats", [P, TS, 6])
        omv = sb("omv", [P, TS, 2])
        orstd = sb("orstd", [P, TS])
        number_u = sb("number_u", [P, 2, TS], U32)

        PLAN_STEPS = 5 + (E - 1) + 1 + 2 * E + (E - 1) + 3
        plan_step = semaphore("plan_step")
        padding_made = semaphore("padding_made")
        padded = semaphore("padded")
        fx_loaded = dma_signal("fx_loaded", 1)
        w1_loaded = dma_signal("w1_loaded", 2)
        sent = dma_signal("sent", TS)
        fln_step = signal("fln_step", 3 * TS)
        fln_rstd = signal("fln_rstd", 2)
        fzT_made = signal("fzT_made", KC)
        fzT_copied = signal("fzT_copied", KC)
        h_made = signal("h_made", MI)
        gelu_done = signal("gelu_done", MI)
        ffn_made = signal("ffn_made", 2)
        zb_made = signal("zb_made", 1)
        xb_made = signal("xb_made", 1)
        numbers_made = signal("numbers_made", 1)
        ysum_made = signal("ysum_made", 2)
        oln_step = signal("oln_step", 3 * TS)
        oln_rstd = signal("oln_rstd", 2)
        final_made = signal("final_made", TS)
        rows_sent = dma_signal("rows_sent", NT)
        rzT_made = signal("rzT_made", 1)
        rzT_copied = signal("rzT_copied", 1)
        logits_made = signal("logits_made", 1)
        rank_made = signal("rank_made", 1)
        ln3_step = signal("ln3_step", 3 * NT)
        ln3_rstd = signal("ln3_rstd", 2)
        route_step = signal("route_step", 6)
        number_made = signal("number_made", 1)
        place_step = signal("place_step", 5)
        consts_in = semaphore("consts_in")
        consts_ready = semaphore("consts_ready")
        CONSTS = 16
        N_WEIGHT_LOADS = 11 + NTERM
        weights_in = semaphore("weights_in")
        x_loaded = dma_signal("x_loaded", 1)
        xres_loaded = dma_signal("xres_loaded", 1)
        ctx_loaded = dma_signal("ctx_loaded", 1)
        q_stored = dma_signal("q_stored", 1)
        k_stored = dma_signal("k_stored", 1)
        q_packed = dma_signal("q_packed", NTERM)
        k_packed = dma_signal("k_packed", NTERM)
        mx_packed = dma_signal("mx_packed", 2)
        cq_stored = dma_signal("cq_stored", 1)
        cq_packed = dma_signal("cq_packed", NTERM)
        cmx_packed = dma_signal("cmx_packed", 2)
        xT_made = signal("xT_made", 1)
        q_made = signal("q_made", 1)
        k_made = signal("k_made", 1)
        v_made = signal("v_made", 1)
        s_made = signal("s_made", 12)
        mxT_made = signal("mxT_made", 1)
        st_made = signal("st_made", 12)
        pv_made = signal("pv_made", 2)
        yt_made = signal("yt_made", 2)
        czT_made = signal("czT_made", 1)
        cq_made = signal("cq_made", 1)
        ckv_made = signal("ckv_made", 1)
        match_made = signal("match_made", 1)
        count_made = signal("count_made", 1)
        cs_made = signal("cs_made", 8)
        cmxT_made = signal("cmxT_made", 1)
        cst_made = signal("cst_made", 8)
        cpv_made = signal("cpv_made", 2)
        cyt_made = signal("cyt_made", 2)
        cyC_made = signal("cyC_made", 1)
        o_made = signal("o_made", 1)
        zT_copied = signal("zT_copied", 1)
        q_high = signal("q_high", 1)
        k_high = signal("k_high", 1)
        q_mid = signal("q_mid", 1)
        k_mid = signal("k_mid", 1)
        exp_done = signal("exp_done", 12)
        mxT_copied = signal("mxT_copied", 1)
        yT_copied = signal("yT_copied", 2)
        czT_copied = signal("czT_copied", 1)
        cq_copied = signal("cq_copied", 1)
        cq_high = signal("cq_high", 1)
        cq_mid = signal("cq_mid", 1)
        ckv_copied = signal("ckv_copied", 2)
        cexp_done = signal("cexp_done", 8)
        cmxT_copied = signal("cmxT_copied", 1)
        cyT_copied = signal("cyT_copied", 2)
        cyC_copied = signal("cyC_copied", 1)
        LN_STEPS = 2 * NT + NT
        ln1_step = signal("ln1_step", LN_STEPS)
        q_rest_made = signal("q_rest_made", 1)
        k_rest_made = signal("k_rest_made", 1)
        v_copied = signal("v_copied", 1)
        max_done = signal("max_done", 12)
        mx_split = signal("mx_split", 2)
        rsum_made = signal("rsum_made", 2)
        y_scaled = signal("y_scaled", 2)
        x1_made = signal("x1_made", 2)
        ln2_step = signal("ln2_step", LN_STEPS)
        cq_rest_made = signal("cq_rest_made", 1)
        match_step = signal("match_step", 2 * NT + 1)
        onehot_made = signal("onehot_made", NT)
        count_copied = signal("count_copied", 1)
        kmask_made = signal("kmask_made", 1)
        vc_made = signal("vc_made", 2)
        cmax_done = signal("cmax_done", 8)
        cmx_split = signal("cmx_split", 2)
        crsum_made = signal("crsum_made", 2)
        cy_scaled = signal("cy_scaled", 2)
        x2_made = signal("x2_made", 1)
        ln1_rstd = signal("ln1_rstd", 2)
        ln2_rstd = signal("ln2_rstd", 2)
        q_low = signal("q_low", 1)
        k_low = signal("k_low", 1)
        cq_low = signal("cq_low", 1)
        kc_step = signal("kc_step", 9)

        passed_sp = semaphore("passed_sp")
        passed_pool = semaphore("passed_pool")
        passed_dve = semaphore("passed_dve")

        def steps(eng, body):
            for i in range(6):
                body(i, i % 2)
            with eng.Fori(6, B, 2) as i:
                body(i, 0)
                body(i + 1, 1)
            for i in range(B, B + LAGS):
                body(i, i % 2)

        def runs(i, lag):
            return not isinstance(i, int) or 0 <= i - lag < B

        def tile_steps(eng, body):
            for k in range(4):
                body(k, k % 2)
            end = TILES - TILES % 2
            with eng.Fori(4, end, 2) as k:
                body(k, 0)
                body(k + 1, 1)
            for k in range(end, TILES + 1):
                body(k, k % 2)

        def tile_runs(k, lag):
            return not isinstance(k, int) or 0 <= k - lag < TILES

        block = stack.enter_context(nc.Block())

        @block.sync
        def _(sp):
            sp.dma_start(consts_sb[:], consts).then_inc(consts_in, 16)
            setup = [
                (wqkv_sb[:], wqkvT.rearrange("(c p) n -> p c n", p=P)),
                (bqk_sb[:], bqkT),
                (bv_sb[:], bv.broadcast_to([P, C])),
                (wq_sb[:], wqT.rearrange("(c p) n -> p c n", p=P)),
                (wc_sb[:], wcT.rearrange("(c p) n -> p c n", p=P)),
                (wo_sb[:], wo.rearrange("(m p) n -> p m n", p=P)),
                (bo_sb[:], bo.broadcast_to([P, C])),
                (gamma_sb[:], gamma.broadcast_to([P, C])),
                (beta_sb[:], beta.broadcast_to([P, C])),
                (wr_sb[:], w_router.rearrange("(c p) n -> p c n", p=P)),
                (wmv_sb[:], wkvT[:, D:2 * D].rearrange("(c p) n -> p c n", p=P)),
            ] + [(wmk_sb[:, :, D * t:D * t + D], wkvT[:, 0:D].rearrange("(c p) n -> p c n", p=P)) for t in range(NTERM)]
            assert len(setup) == N_WEIGHT_LOADS
            for dst, src in setup:
                sp.dma_start(dst, src).then_inc(weights_in, 16)

            def load_x(b, par):
                if begun(b - 2):
                    sp.wait_ge(ln1_step.sem, ln1_step.value(b - 2))
                    sp.sem_inc(passed_sp, 1)
                sp.dma_start(x_in[:, par], x[bass.ds(b % B, 1)].rearrange("o (t p) c -> p (o t) c", p=P)).then_inc(x_loaded[par].sem, 16)

            def store_parts(b, par, name, parts, low, stored):
                sp.wait_ge(low.sem, low.value(b))
                sp.sem_inc(passed_sp, 1)
                sp.dma_start(parts_dram[name][par].rearrange("y h d n -> (h d) y n"), parts[:]).then_inc(stored[par].sem, 16)

            def pack(b, par, name, stored, packed, dst, reader):
                sp.wait_ge(stored[par].sem, stored[par].value(b // 2))
                sp.sem_inc(passed_sp, 1)
                if begun(b - 2):
                    sp.wait_ge(reader.sem, reader.value(b - 2))
                    sp.sem_inc(passed_sp, 1)
                for t, part in enumerate(K_PARTS if name == "k" else Q_PARTS):
                    sp.dma_start(dst[D * t:D * t + D, par].rearrange("d (h c) n -> d h (c n)", h=HP),
                                 parts_dram[name][par, part].rearrange("h d n -> d h n")).then_inc(packed[par].sem, 16)

            def pack_max(b, par, copied, packed, src, dst, row):
                sp.wait_ge(copied.sem, copied.value(b))
                sp.sem_inc(passed_sp, 1)
                for part in range(2):
                    sp.dma_start(dst[row + part:row + part + 1, par], src[H * part:H * part + H, :]).then_inc(packed[par].sem, 16)

            def body(i, par):
                if runs(i, 0):
                    if isinstance(i, int) and i == 0:
                        load_x(0, 0)
                    load_x(i + 1, 1 - par)
                if runs(i, 1):
                    if begun(i - 3):
                        sp.wait_ge(x1_made.sem, x1_made.value(i - 3))
                        sp.sem_inc(passed_sp, 1)
                    sp.dma_start(x_res[:, 1 - par], x[bass.ds(i - 1, 1)].rearrange("o (t p) c -> p (o t) c", p=P)).then_inc(xres_loaded[1 - par].sem, 16)
                    if begun(i - 3):
                        sp.wait_ge(match_made.sem, match_made.value(i - 3))
                        sp.sem_inc(passed_sp, 1)
                    sp.dma_start(ctx_sb[:, 1 - par], ctxT[bass.ds(i - 1, 1)].rearrange("o (c p) m -> p (o c) m", p=P)).then_inc(ctx_loaded[1 - par].sem, 16)
                if runs(i, 1):
                    pack_max(i - 1, 1 - par, mxT_copied, mx_packed, mxT, QP, KR)
                if runs(i, 2):
                    pack_max(i - 2, par, cmxT_copied, cmx_packed, cmxT, QC, KR + 1)
                if runs(i, 0):
                    store_parts(i, par, "q", q_parts, q_low, q_stored)
                    store_parts(i, par, "k", k_parts, k_low, k_stored)
                    pack(i, par, "q", q_stored, q_packed, QP, st_made)
                    pack(i, par, "k", k_stored, k_packed, KP, st_made)
                if runs(i, 1):
                    store_parts(i - 1, 1 - par, "qc", cq_parts, cq_low, cq_stored)
                    pack(i - 1, 1 - par, "qc", cq_stored, cq_packed, QC, cst_made)

            steps(sp, body)
            sp.wait_ge(x_loaded[0].sem, x_loaded[0].value(B // 2))
            sp.sem_inc(passed_sp, 1)

            for b in (B - 2, B - 1):
                sp.wait_ge(rows_sent[b % 2].sem, rows_sent[b % 2].value(b // 2))
                sp.sem_inc(passed_sp, 1)
            sp.wait_ge(plan_step, PLAN_STEPS)
            sp.wait_ge(padding_made, 2)
            sp.wait_ge(st_made.sem, st_made.value(B - 1))
            sp.sem_inc(passed_sp, 1)
            for e in range(E):
                start = sp.value_load(next_u[0:1, e:e + 1], min_val=e * ROOM, max_val=e * ROOM + B * T)
                sp.dma_start(rows_dram[bass.ds(start, TILE)].rearrange("(p j) c -> p (j c)", p=P), padding[:].rearrange("p j c -> p (j c)")).then_inc(padded, 16)
            sp.dma_start(rows_dram[E * ROOM:E * ROOM + TILE].rearrange("(p j) c -> p (j c)", p=P), padding[:].rearrange("p j c -> p (j c)")).then_inc(padded, 16)
            sp.wait_ge(padded, 16 * (E + 1))

            def load_tile(k, par):
                if not tile_runs(k, 0):
                    return
                row = sp.value_load(tile_row_u[0:1, bass.ds(k, 1)], min_val=0, max_val=E * ROOM)
                expert = sp.value_load(tile_expert_u[0:1, bass.ds(k, 1)], min_val=0, max_val=E - 1)
                if begun(k - 2):
                    sp.wait_ge(fln_step.sem, fln_step.value(k - 2))
                    sp.sem_inc(passed_sp, 1)
                    sp.wait_ge(xb_made.sem, xb_made.value(k - 2))
                    sp.sem_inc(passed_sp, 1)
                    sp.wait_ge(numbers_made.sem, numbers_made.value(k - 2))
                    sp.sem_inc(passed_sp, 1)
                sp.dma_start(fx[:, par].rearrange("p j c -> p (j c)"), rows_dram[bass.ds(row, TILE)].rearrange("(p j) c -> p (j c)", p=P)).then_inc(fx_loaded[par].sem, 16)
                if begun(k - 2):
                    sp.wait_ge(gelu_done.sem, gelu_done.value(k - 2))
                    sp.sem_inc(passed_sp, 1)
                sp.dma_start(w1_sb[:, par], w1[bass.ds(expert, 1)].rearrange("o (c p) i -> p (o c) i", p=P)).then_inc(w1_loaded[par].sem, 16)
                sp.dma_start(b1_sb[:, par], b1T[bass.ds(expert, 1)].rearrange("o p m -> p (o m)")).then_inc(w1_loaded[par].sem, 16)

            tile_steps(sp, load_tile)

        @block.tensor
        def _(pe):
            def latest(*readers):
                for sig, b, k in readers:
                    if not isinstance(b, int) or 0 <= b < B:
                        return sig.sem, sig.value(b, k)
                return consts_ready, CONSTS

            def transpose(dst, src, identity):
                return pe.transpose(dst, src, identity)

            def project(bank, lhs, rhs, n_out, width):
                for m in range(n_out):
                    for kc in range(KC):
                        last = pe.matmul(psum[:, bank, m * width:(m + 1) * width], lhs(kc, m), rhs(kc), start=(kc == 0), stop=(kc == KC - 1))
                return last

            def turn_z(i, lag, bank, src, ready, free, made):
                pe.wait_ge(*free)
                pe.wait_ge(ready.sem, ready.value(i - lag))
                for c in range(KC):
                    for t in range(NT):
                        last = transpose(psum[:, bank, c * T + t * P:c * T + (t + 1) * P], src[:, t, c * P:(c + 1) * P], ident)
                last.then_inc(made.sem, 1)

            def project_q(i, par):
                pe.wait_ge(zT_copied.sem, zT_copied.value(i))
                pe.wait_ge(*latest((cy_scaled, i - 3, 1), (match_step, i - 2, 2 * NT), (q_rest_made, i - 1, 1)))
                project(4, lambda kc, m: wqkv_sb[:, kc, m * P:(m + 1) * P], lambda kc: zT[:, kc, :], KC, T).then_inc(q_made.sem, 1)

            def project_k(i, par):
                pe.wait_ge(*latest((cy_scaled, i - 3, 2), (kmask_made, i - 2, 1), (k_rest_made, i - 1, 1)))
                project(5, lambda kc, m: wqkv_sb[:, kc, C + m * P:C + (m + 1) * P], lambda kc: zT[:, kc, :], KC, T).then_inc(k_made.sem, 1)

            def project_v(i, par):
                pe.wait_ge(*latest((cyC_copied, i - 3, 1), (y_scaled, i - 2, 1), (v_copied, i - 1, 1)))
                project(6, lambda kc, m: zT[:, kc, m * P:(m + 1) * P], lambda kc: wqkv_sb[:, kc, 2 * C:3 * C], NT, C).then_inc(v_made.sem, 1)

            def stage_B(i, par):
                b, q = i - 1, 1 - par
                pe.wait_ge(q_packed[q].sem, q_packed[q].value(b // 2))
                pe.wait_ge(k_packed[q].sem, k_packed[q].value(b // 2))
                for n in range(12):
                    bank = S_BANKS[n % 2]
                    if n >= 2:
                        pe.wait_ge(max_done.sem, max_done.value(b, n - 1))
                    else:
                        pe.wait_ge(*latest(((cq_copied, czT_copied)[n], i - 2, 1)))
                    if n < 4:
                        for j in range(4):
                            h = 4 * n + j
                            pe.matmul(psum[:, bank, j * P:(j + 1) * P], QP[0:KR, q, h, 0:P], KP[0:KR, q, h, 0:P], start=(j == 0), stop=False, skip_group_check=True)
                        diagonal = psum[:, bank, :]
                        masks = 4
                    else:
                        for j in range(2):
                            h = 2 * (n - 4) + j
                            pe.matmul(psum[:, bank, j * T:(j + 1) * T], QP[0:KR, q, h, P:T], KP[0:KR, q, h, :], start=(j == 0), stop=False, skip_group_check=True)
                        diagonal = psum[:, bank, :].rearrange("p (j k) -> p j k", j=2)[:, :, P:T]
                        masks = 2
                    pe.matmul(diagonal, ident_bf[:], mask_s[:].unsqueeze(1).broadcast_to([P, masks, P]), start=False, stop=True, skip_group_check=True).then_inc(s_made.sem, 1)

            def turn_max(i, lag, split, free, made, mx, bank):
                pe.wait_ge(*free)
                pe.wait_ge(split.sem, split.value(i - lag))
                for t in range(NT):
                    last = transpose(psum[0:2 * H, bank, 0:T // 2].bitcast(BF16)[:, t * P:(t + 1) * P], mx[:, t].rearrange("p y h -> p (y h)"), ident_bf[:])
                last.then_inc(made.sem, 1)

            def stage_C(i, par):
                b, q = i - 1, 1 - par
                pe.wait_ge(mx_packed[q].sem, mx_packed[q].value(b // 2))
                KS = KR + 2

                def scores(n):
                    g, r = divmod(n, 3)
                    bank = ST_BANKS[n % 2]
                    if n >= 2:
                        pe.wait_ge(exp_done.sem, exp_done.value(b, n - 1))
                    elif n == 0:
                        pe.wait_ge(*latest((zT_copied, i, 1), (cexp_done, i - 3, 7)))
                    else:
                        pe.wait_ge(*latest((x2_made, i - 3, 1), (exp_done, i - 2, 12)))
                    if r < 2:
                        for j in range(2):
                            h = 4 * g + 2 * r + j
                            pe.matmul(psum[:, bank, j * T:(j + 1) * T], KP[0:KS, q, h, 0:P], QP[0:KS, q, h, :], start=(j == 0), stop=False, skip_group_check=True)
                        diagonal = psum[:, bank, :].rearrange("p (j k) -> p j k", j=2)[:, :, 0:P]
                        masks = 2
                    else:
                        for j in range(4):
                            h = 4 * g + j
                            pe.matmul(psum[:, bank, j * P:(j + 1) * P], KP[0:KS, q, h, P:T], QP[0:KS, q, h, P:T], start=(j == 0), stop=False, skip_group_check=True)
                        diagonal = psum[:, bank, :]
                        masks = 4
                    pe.matmul(diagonal, ident_bf[:], mask_t[:].unsqueeze(1).broadcast_to([P, masks, P]), start=False, stop=True, skip_group_check=True).then_inc(st_made.sem, 1)

                def values(g):
                    bank, col = Y_BANKS[g // 2], (g % 2) * T
                    if g == 0:
                        pe.wait_ge(*latest((q_rest_made, i, 1), (cy_scaled, i - 3, 1)))
                    elif g == 2:
                        pe.wait_ge(*latest((k_rest_made, i, 1), (cy_scaled, i - 3, 2)))
                    pe.wait_ge(exp_done.sem, exp_done.value(b, 3 * g + 3))
                    for j in range(4):
                        pe.matmul(psum[32 * j:32 * j + 32, bank, col:col + T], V[:, q, 0, 4 * g + j, :], PA[:, 4 * g + j, :], start=True, stop=False, skip_group_check=True)
                    for j in range(4):
                        last = pe.matmul(psum[32 * j:32 * j + 32, bank, col + P:col + T], V[:, q, 1, 4 * g + j, :], PB[:, 4 * g + j, :], start=False, stop=True, skip_group_check=True)
                    if g % 2 == 1:
                        last.then_inc(pv_made.sem, 1)

                pe.wait_ge(v_copied.sem, v_copied.value(b))
                for n in range(3):
                    scores(n)
                for g in range(4):
                    if g < 3:
                        for n in range(3 * g + 3, 3 * g + 6):
                            scores(n)
                    values(g)

            def turn_y(i, lag, copied, free, made, src, banks):
                pe.wait_ge(copied.sem, copied.value(i - lag))
                for t in range(NT):
                    pe.wait_ge(*free[t])
                    for g in range(H // 4):
                        last = transpose(psum[:, banks[t], g * P:(g + 1) * P], src[:, g, t * P:(t + 1) * P], ident)
                    last.then_inc(made.sem, 1)

            def project_ctx(i, par):
                b, q = i - 1, 1 - par
                pe.wait_ge(ctx_loaded[q].sem, ctx_loaded[q].value(b // 2))
                pe.wait_ge(mxT_copied.sem, mxT_copied.value(b))
                for kc in range(KC):
                    pe.matmul(psum[0:KR, 0, 0:M], wmk_sb[:, kc, :], ctx_sb[:, q, kc, :], start=(kc == 0), stop=(kc == KC - 1))
                for kc in range(KC):
                    last = pe.matmul(psum[0:M, 0, P:P + D], ctx_sb[:, q, kc, :], wmv_sb[:, kc, :], start=(kc == 0), stop=(kc == KC - 1))
                last.then_inc(ckv_made.sem, 1)

            def project_cq(i, par):
                if begun(i - 1):
                    pe.wait_ge(czT_copied.sem, czT_copied.value(i - 1))
                pe.wait_ge(ckv_copied.sem, ckv_copied.value(i - 1))
                project(0, lambda kc, m: wq_sb[:, kc, m * P:(m + 1) * P], lambda kc: czT[:, kc, :], KC, T).then_inc(cq_made.sem, 1)

            def match(i, par):
                pe.wait_ge(*latest((cyT_copied, i - 3, 1), (yT_copied, i - 2, 1)))
                if begun(i - 2):
                    pe.wait_ge(cq_copied.sem, cq_copied.value(i - 2))
                project(4, lambda kc, m: cqT[:, kc * T + m * P:kc * T + (m + 1) * P], lambda kc: ctx_sb[:, par, kc, :], NT, M).then_inc(match_made.sem, 1)

            def counts(i, par):
                b = i - 2
                pe.wait_ge(*latest((cyT_copied, i - 3, 2), (yT_copied, i - 2, 2)))
                pe.wait_ge(onehot_made.sem, onehot_made.value(b))
                for t in range(NT):
                    pe.matmul(psum[0:M, 5, 0:1], onehot[:, t, :], ones_bf[:, 0:1], start=(t == 0), stop=(t == NT - 1))
                for t in range(NT):
                    last = pe.matmul(psum[:, 5, P:P + M], ones_bf[:], onehot[:, t, :], start=(t == 0), stop=(t == NT - 1))
                last.then_inc(count_made.sem, 1)

            def stage_E(i, par):
                b = i - 2
                pe.wait_ge(cq_packed[par].sem, cq_packed[par].value(b // 2))
                pe.wait_ge(kmask_made.sem, kmask_made.value(b))
                pe.wait_ge(kc_step.sem, kc_step.value(b))
                KS = KR + 1
                for n in range(8):
                    t, g = divmod(n, 4)
                    bank = S_BANKS[n % 2]
                    if n >= 2:
                        pe.wait_ge(cmax_done.sem, cmax_done.value(b, n - 1))
                    else:
                        pe.wait_ge(*latest((max_done, i - 1, 11 + n), ((cq_copied, czT_copied)[n], i - 2, 1)))
                    for j in range(4):
                        last = pe.matmul(psum[:, bank, j * M:(j + 1) * M], QC[0:KS, par, 4 * g + j, t * P:(t + 1) * P], KCx[0:KS, par, 0:M], start=True, stop=True)
                    last.then_inc(cs_made.sem, 1)

            def stage_F1(i, par):
                b = i - 2
                pe.wait_ge(cmx_packed[par].sem, cmx_packed[par].value(b // 2))
                pe.wait_ge(vc_made.sem, vc_made.value(b))
                KS = KR + 3

                def scores(n):
                    bank = ST_BANKS[n % 2]
                    if n >= 2:
                        pe.wait_ge(cexp_done.sem, cexp_done.value(b, n - 1))
                    elif n == 0:
                        pe.wait_ge(*latest((exp_done, i - 1, 11), (cexp_done, i - 3, 7)))
                    else:
                        pe.wait_ge(*latest((exp_done, i - 1, 12), (x2_made, i - 3, 1)))
                    last = pe.matmul(psum[0:M, bank, :], KCx[0:KS, par, 0:M], QC[0:KS, par, 2 * n:2 * n + 2, :], start=True, stop=True)
                    last.then_inc(cst_made.sem, 1)

                def values(g):
                    bank, col = Y_BANKS[g // 2], (g % 2) * T
                    if g % 2 == 0:
                        pe.wait_ge(*latest((yT_copied, i - 1, g // 2 + 1), (cy_scaled, i - 3, g // 2 + 1)))
                    pe.wait_ge(cexp_done.sem, cexp_done.value(b, 2 * g + 2))
                    for j in range(4):
                        last = pe.matmul(psum[32 * j:32 * j + 32, bank, col:col + T], VC[0:M, par, :], PC[0:M, 4 * g + j, :], start=True, stop=True)
                    if g % 2 == 1:
                        last.then_inc(cpv_made.sem, 1)

                scores(0)
                scores(1)
                for g in range(4):
                    if g < 3:
                        scores(2 * g + 2)
                        scores(2 * g + 3)
                    values(g)

            def project_out(i, par):
                b = i - 3
                pe.wait_ge(cexp_done.sem, cexp_done.value(b))
                pe.wait_ge(cyC_copied.sem, cyC_copied.value(b))
                project(3, lambda kc, m: cyC[:, kc, m * P:(m + 1) * P], lambda kc: wc_sb[:, kc, :], NT, C).then_inc(o_made.sem, 1)

            def logits(i, par):
                b = i - 4
                pe.wait_ge(*latest((y_scaled, i - 2, 2), (place_step, i - 5, 5)))
                pe.wait_ge(rzT_copied.sem, rzT_copied.value(b))
                for t in range(NT):
                    for kc in range(KC):
                        last = pe.matmul(psum[:, 7, t * E:(t + 1) * E], rzT[:, kc, t * P:(t + 1) * P], wr_sb[:, kc, :], start=(kc == 0), stop=(kc == KC - 1))
                last.then_inc(logits_made.sem, 1)

            def rank(i, par):
                b = i - 4
                pe.wait_ge(route_step.sem, route_step.value(b))
                pe.matmul(psum[:, 7, 0:E], before_bf[:], chosen_bf[:, 0, :], start=True, stop=True)
                pe.matmul(psum[:, 7, E:2 * E], before_bf[:], chosen_bf[:, 1, :], start=True, stop=False)
                pe.matmul(psum[:, 7, E:2 * E], ones_bf[:], chosen_bf[:, 0, :], start=False, stop=True)
                pe.matmul(psum[:, 7, 2 * E:3 * E], ones_bf[:], chosen_bf[:, 0, :], start=True, stop=False)
                pe.matmul(psum[:, 7, 2 * E:3 * E], ones_bf[:], chosen_bf[:, 1, :], start=False, stop=True).then_inc(rank_made.sem, 1)

            def body(i, par):
                if runs(i, 2):
                    match(i, par)
                if runs(i, 1):
                    stage_B(i, par)
                if runs(i, 4):
                    turn_z(i, 4, 6, rz, ln3_step, latest((y_scaled, i - 2, 1), (cyC_copied, i - 4, 1)), rzT_made)
                if runs(i, 2):
                    counts(i, par)
                if runs(i, 3):
                    turn_y(i, 3, cyT_copied, (latest((match_step, i - 2, 2 * NT), (cyT_copied, i - 3, 1)), latest((kmask_made, i - 2, 1), (cyT_copied, i - 3, 2))), cyt_made, cyT, (4, 5))
                if runs(i, 4):
                    logits(i, par)
                if runs(i, 2):
                    stage_E(i, par)
                if runs(i, 3):
                    turn_z(i, 3, 6, cy, cy_scaled, latest((rzT_copied, i - 4, 1), (y_scaled, i - 2, 1)), cyC_made)
                if runs(i, 0):
                    turn_z(i, 0, 2, z, ln1_step, latest((cexp_done, i - 3, 7), (exp_done, i - 2, 11), (zT_copied, i - 1, 1)), xT_made)
                if runs(i, 3):
                    project_out(i, par)
                if runs(i, 0):
                    project_q(i, par)
                    project_k(i, par)
                if runs(i, 4):
                    rank(i, par)
                if runs(i, 0):
                    project_v(i, par)
                if runs(i, 1):
                    turn_max(i, 1, mx_split, latest((cmax_done, i - 2, 7), (max_done, i - 1, 11)), mxT_made, mx2, 0)
                if runs(i, 2):
                    turn_max(i, 2, cmx_split, latest((cmax_done, i - 2, 8)), cmxT_made, cmx2, 1)
                if runs(i, 1):
                    stage_C(i, par)
                    project_ctx(i, par)
                    turn_y(i, 1, yT_copied, (latest((v_copied, i, 1), (cyC_copied, i - 3, 1)), latest((place_step, i - 4, 5), (y_scaled, i - 2, 2))), yt_made, yT, (6, 7))
                if runs(i, 2):
                    stage_F1(i, par)
                if runs(i, 1):
                    turn_z(i, 1, 1, cz, ln2_step, latest((cmxT_copied, i - 2, 1), (max_done, i - 1, 12)), czT_made)
                    project_cq(i, par)

            pe.wait_ge(consts_ready, CONSTS)
            pe.wait_ge(weights_in, 16 * N_WEIGHT_LOADS)
            steps(pe, body)

            pe.wait_ge(place_step.sem, place_step.value(B - 1))
            pe.wait_ge(cq_rest_made.sem, cq_rest_made.value(B - 1))
            pe.wait_ge(cexp_done.sem, cexp_done.value(B - 1))

            def turn_tile(k, par):
                pe.wait_ge(fln_step.sem, fln_step.value(k))
                for kc in range(KC):
                    if begun(k - 1):
                        pe.wait_ge(fzT_copied.sem, fzT_copied.value(k - 1, kc + 1))
                    for j in range(TS):
                        last = transpose(psum[:, 6 + kc, j * P:(j + 1) * P], fz[:, j, kc * P:(kc + 1) * P], ident)
                    last.then_inc(fzT_made.sem, 1)

            def widen(k, par):
                b, q = k - 1, 1 - par
                pe.wait_ge(w1_loaded[q].sem, w1_loaded[q].value(b // 2))
                pe.wait_ge(fzT_copied.sem, fzT_copied.value(b))
                for m in range(MI):
                    bank = m % 4
                    if m >= 4:
                        pe.wait_ge(gelu_done.sem, gelu_done.value(b, m - 3))
                    elif begun(b - 1):
                        pe.wait_ge(gelu_done.sem, gelu_done.value(b - 1, m + 5))
                    for kc in range(KC):
                        last = pe.matmul(psum[:, bank, :], w1_sb[:, q, kc, m * P:(m + 1) * P], fzT[:, kc, :], start=(kc == 0), stop=(kc == KC - 1))
                    last.then_inc(h_made.sem, 1)

            def narrow(k, par):
                b = k - 1
                for half in range(2):
                    if begun(b - 1):
                        pe.wait_ge(ysum_made.sem, ysum_made.value(b - 1, half + 1))
                    for j in range(2):
                        for m in range(MI):
                            if half == 0 and j == 0:
                                pe.wait_ge(gelu_done.sem, gelu_done.value(b, m + 1))
                            t = 2 * half + j
                            last = pe.matmul(psum[:, 4 + half, j * C:(j + 1) * C], hT[:, m, t * P:(t + 1) * P], wo_sb[:, m, :], start=(m == 0), stop=(m == MI - 1))
                    last.then_inc(ffn_made.sem, 1)

            def tile_body(k, par):
                if tile_runs(k, 1):
                    widen(k, par)
                if tile_runs(k, 0):
                    turn_tile(k, par)
                if tile_runs(k, 1):
                    narrow(k, par)

            tile_steps(pe, tile_body)

        @block.scalar
        def _(act):
            def copy(dst, src):
                return act.activation(dst, src, ACT.Copy)

            def copy_z(i, lag, made, free, dst, bank, copied):
                act.wait_ge(made.sem, made.value(i - lag))
                if begun(i - lag - 1):
                    act.wait_ge(free.sem, free.value(i - lag - 1))
                copy(dst[:].rearrange("p c n -> p (c n)"), psum[:, bank, :]).then_inc(copied.sem, 1)

            def stage_A(i, par):
                for made, stored, parts, high, bank, bias in ((q_made, q_stored, q_parts, q_high, 4, 0), (k_made, k_stored, k_parts, k_high, 5, KC)):
                    act.wait_ge(made.sem, made.value(i))
                    if begun(i - 1):
                        act.wait_ge(stored[1 - par].sem, stored[1 - par].value((i - 1) // 2))
                    for c in range(KC):
                        last = act.activation(parts[:, 0, c * T:(c + 1) * T], psum[:, bank, c * T:(c + 1) * T], ACT.Identity, bias=bqk_sb[:, bias + c:bias + c + 1])
                    last.then_inc(high.sem, 1)
                for made, parts, rest, mid in ((q_rest_made, q_parts, q_rest, q_mid), (k_rest_made, k_parts, k_rest, k_mid)):
                    act.wait_ge(made.sem, made.value(i))
                    copy(parts[:, 1, :], rest[:]).then_inc(mid.sem, 1)

            def copy_max(b, par, made, packed, dst, bank, copied):
                act.wait_ge(made.sem, made.value(b))
                if begun(b - 1):
                    act.wait_ge(packed[1 - par].sem, packed[1 - par].value((b - 1) // 2))
                copy(dst[:], psum[0:2 * H, bank, 0:T // 2].bitcast(BF16)).then_inc(copied.sem, 1)

            def stage_C(i, par):
                b = i - 1
                if begun(b - 1):
                    act.wait_ge(pv_made.sem, pv_made.value(b - 1))
                for n in range(12):
                    g, r = divmod(n, 3)
                    act.wait_ge(st_made.sem, st_made.value(b, n + 1))
                    if r < 2:
                        h = 4 * g + 2 * r
                        dst = PA[:, h:h + 2, :].rearrange("p h n -> p (h n)")
                    else:
                        dst = PB[:, 4 * g:4 * g + 4, :].rearrange("p h n -> p (h n)")
                    act.activation(dst, psum[:, ST_BANKS[n % 2], :], ACT.Exp, scale=D ** -0.5).then_inc(exp_done.sem, 1)
                if begun(b - 1):
                    act.wait_ge(yt_made.sem, yt_made.value(b - 1))
                for n in range(2):
                    act.wait_ge(pv_made.sem, pv_made.value(b, n + 1))
                    copy(yT[:, 2 * n:2 * n + 2, :].rearrange("p g n -> p (g n)"), psum[:, Y_BANKS[n], :]).then_inc(yT_copied.sem, 1)

            def stage_F1(i, par):
                b = i - 2
                if begun(b - 1):
                    act.wait_ge(cpv_made.sem, cpv_made.value(b - 1))
                for n in range(8):
                    act.wait_ge(cst_made.sem, cst_made.value(b, n + 1))
                    act.activation(PC[0:M, 2 * n:2 * n + 2, :].rearrange("p h n -> p (h n)"), psum[0:M, ST_BANKS[n % 2], :], ACT.Exp, scale=D ** -0.5).then_inc(cexp_done.sem, 1)
                if begun(b - 1):
                    act.wait_ge(cyt_made.sem, cyt_made.value(b - 1))
                for n in range(2):
                    act.wait_ge(cpv_made.sem, cpv_made.value(b, n + 1))
                    copy(cyT[:, 2 * n:2 * n + 2, :].rearrange("p g n -> p (g n)"), psum[:, Y_BANKS[n], :]).then_inc(cyT_copied.sem, 1)

            def copy_ctx(i, par):
                b = i - 1
                act.wait_ge(ckv_made.sem, ckv_made.value(b))
                if begun(b - 1):
                    act.wait_ge(kc_step.sem, kc_step.value(b - 1))
                if begun(b - 1):
                    act.wait_ge(vc_made.sem, vc_made.value(b - 1))
                copy(kc32[0:KR, :], psum[0:KR, 0, 0:M]).then_inc(ckv_copied.sem, 1)
                copy(cv[0:M, :], psum[0:M, 0, P:P + D]).then_inc(ckv_copied.sem, 1)

            def stage_D(i, par):
                b = i - 1
                act.wait_ge(cq_made.sem, cq_made.value(b))
                if begun(b - 1):
                    act.wait_ge(match_made.sem, match_made.value(b - 1))
                    act.wait_ge(cq_rest_made.sem, cq_rest_made.value(b - 1))
                copy(cqT[:], psum[:, 0, :]).then_inc(cq_copied.sem, 1)
                act.wait_ge(cq_copied.sem, cq_copied.value(b))
                if begun(b - 1):
                    act.wait_ge(cq_stored[par].sem, cq_stored[par].value((b - 1) // 2))
                copy(cq_parts[:, 0, :], cqT[:]).then_inc(cq_high.sem, 1)
                act.wait_ge(cq_rest_made.sem, cq_rest_made.value(b))
                copy(cq_parts[:, 1, :], cq_rest[:]).then_inc(cq_mid.sem, 1)

            def body(i, par):
                if runs(i, 4):
                    copy_z(i, 4, rzT_made, logits_made, rzT, 6, rzT_copied)
                if runs(i, 3):
                    copy_z(i, 3, cyC_made, o_made, cyC, 6, cyC_copied)
                if runs(i, 0):
                    copy_z(i, 0, xT_made, v_made, zT, 2, zT_copied)
                    stage_A(i, par)
                if runs(i, 1):
                    copy_max(i - 1, 1 - par, mxT_made, mx_packed, mxT, 0, mxT_copied)
                if runs(i, 2):
                    copy_max(i - 2, par, cmxT_made, cmx_packed, cmxT, 1, cmxT_copied)
                if runs(i, 1):
                    stage_C(i, par)
                    copy_ctx(i, par)
                if runs(i, 2):
                    stage_F1(i, par)
                if runs(i, 1):
                    copy_z(i, 1, czT_made, cq_made, czT, 1, czT_copied)
                    stage_D(i, par)

            act.wait_ge(weights_in, 16 * N_WEIGHT_LOADS)
            steps(act, body)

            act.wait_ge(pv_made.sem, pv_made.value(B - 1))
            act.wait_ge(cst_made.sem, cst_made.value(B - 1))

            def tile_body(k, par):
                if tile_runs(k, 1):
                    b, q = k - 1, 1 - par
                    act.wait_ge(w1_loaded[q].sem, w1_loaded[q].value(b // 2))
                    if begun(b - 1):
                        act.wait_ge(ffn_made.sem, ffn_made.value(b - 1))
                    for m in range(MI):
                        act.wait_ge(h_made.sem, h_made.value(b, m + 1))
                        act.activation(hT[:, m, :], psum[:, m % 4, :], ACT.Gelu, bias=b1_sb[:, q, m:m + 1]).then_inc(gelu_done.sem, 1)
                if tile_runs(k, 0):
                    if begun(k - 1):
                        act.wait_ge(h_made.sem, h_made.value(k - 1))
                    for kc in range(KC):
                        act.wait_ge(fzT_made.sem, fzT_made.value(k, kc + 1))
                        copy(fzT[:, kc, :], psum[:, 6 + kc, :]).then_inc(fzT_copied.sem, 1)

            tile_steps(act, tile_body)

        @block.vector
        def _(dve):
            made = [0]

            def constant(ins):
                ins.then_inc(consts_ready, 1)
                made[0] += 1

            dve.wait_ge(consts_in, 16)
            constant(dve.tensor_copy(ident_bf[:], consts_sb[:, 0:P]))
            constant(dve.tensor_copy(mask_s[:], consts_sb[:, P:2 * P]))
            constant(dve.tensor_copy(mask_t[:], consts_sb[:, 2 * P:3 * P]))
            constant(dve.memset(ones_bf[:], 1.0))
            constant(dve.tensor_copy(before_bf[:], consts_sb[:, BEFORE:BEFORE + P]))
            constant(dve.tensor_copy(next_row[:], consts_sb[:, NEXT_ROW:NEXT_ROW + E]))
            for par in range(2):
                constant(dve.tensor_copy(x2[:, par, :, C], consts_sb[:, NUMBERS + par * NT:NUMBERS + (par + 1) * NT]))
            constant(dve.memset(minus_half[:], -0.5))
            constant(dve.memset(V[:], 0.0))
            constant(dve.memset(VC[:], 0.0))
            constant(dve.memset(KP[KR:P], 1.0))
            constant(dve.memset(QC[KR:KR + 1], 1.0))
            constant(dve.memset(KCx[KR:P], 1.0))
            dve.wait_ge(consts_ready, 10)
            constant(dve.memset(V[:, 0, :, :, D:D + 1], 1.0))
            constant(dve.memset(V[:, 1, :, :, D:D + 1], 1.0))
            dve.wait_ge(consts_ready, made[0])
            dve.wait_ge(weights_in, 16 * N_WEIGHT_LOADS)
            assert made[0] == CONSTS

            def layer_norm(b, src, dst, st, mean_var, step, rs, rstd_made, NT=NT):
                for t in range(NT):
                    dve.bn_stats(st[:, t, :], src[:, t, :]).then_inc(step.sem, 1)
                for t in range(NT):
                    dve.wait_ge(step.sem, step.value(b, t + 1))
                    dve.sem_inc(passed_dve, 1)
                    dve.bn_aggr(mean_var[:, t, :], st[:, t, :]).then_inc(step.sem, 1)
                dve.wait_ge(rstd_made.sem, rstd_made.value(b))
                for t in range(NT):
                    dve.tensor_scalar(dst[:, t, :], src[:, t, :], mean_var[:, t, 0:1], rs[:, t:t + 1], ALU.subtract, ALU.mult).then_inc(step.sem, 1)

            def split_max(b, done, top, mx, turned, split):
                dve.wait_ge(done.sem, done.value(b))
                if begun(b - 1):
                    dve.wait_ge(turned.sem, turned.value(b - 1))
                dve.tensor_scalar(mx[:, :, 0, :], top[:], -1.0, None, ALU.mult).then_inc(split.sem, 1)
                dve.wait_ge(split.sem, split.value(b, 1))
                dve.scalar_tensor_tensor(mx[:, :, 1, :], top[:], -1.0, mx[:, :, 0, :], ALU.mult, ALU.subtract).then_inc(split.sem, 1)

            def stage_B(i, par):
                b = i - 1
                for n in range(12):
                    dve.wait_ge(s_made.sem, s_made.value(b, n + 1))
                    bank = psum[:, S_BANKS[n % 2], :]
                    if n < 4:
                        dve.tensor_reduce(negmax[:, 0, 4 * n:4 * n + 4], bank.rearrange("p (h k) -> p h k", h=4), AX_X, ALU.max).then_inc(max_done.sem, 1)
                    else:
                        h = 2 * (n - 4)
                        dve.tensor_reduce(negmax[:, 1, h:h + 2], bank.rearrange("p (h k) -> p h k", h=2), AX_X, ALU.max).then_inc(max_done.sem, 1)
                split_max(b, max_done, negmax, mx2, mxT_made, mx_split)

            def stage_E(i, par):
                b = i - 2
                for n in range(8):
                    t, g = divmod(n, 4)
                    dve.wait_ge(cs_made.sem, cs_made.value(b, n + 1))
                    dve.tensor_reduce(cnegmax[:, t, 4 * g:4 * g + 4], psum[:, S_BANKS[n % 2], 0:4 * M].rearrange("p (h k) -> p h k", h=4), AX_X, ALU.max).then_inc(cmax_done.sem, 1)
                split_max(b, cmax_done, cnegmax, cmx2, cmxT_made, cmx_split)

            def stage_A1(i, par):
                dve.wait_ge(x_loaded[par].sem, x_loaded[par].value(i // 2))
                if begun(i - 1):
                    dve.wait_ge(xT_made.sem, xT_made.value(i - 1))
                layer_norm(i, x_in[:, par], z, stats, mv, ln1_step, rstd, ln1_rstd)

            def stage_A2(i, par):
                for high, low, mid, parts, rest, bank, bias, rest_made in ((q_high, q_low, q_mid, q_parts, q_rest, 4, 0, q_rest_made), (k_high, k_low, k_mid, k_parts, k_rest, 5, KC, k_rest_made)):
                    dve.wait_ge(high.sem, high.value(i))
                    if begun(i - 1):
                        dve.wait_ge(low.sem, low.value(i - 1))
                        dve.wait_ge(mid.sem, mid.value(i - 1))
                    for c in range(KC):
                        cols = slice(c * T, (c + 1) * T)
                        last = dve.scalar_tensor_tensor(rest[:, cols], psum[:, bank, cols], bqk_sb[:, bias + c:bias + c + 1], parts[:, 0, cols], ALU.add, ALU.subtract)
                    last.then_inc(rest_made.sem, 1)

            def add_v_bias(i, par):
                dve.wait_ge(v_made.sem, v_made.value(i))
                if begun(i - 2):
                    dve.wait_ge(pv_made.sem, pv_made.value(i - 2))
                for t in range(NT):
                    last = dve.tensor_tensor(V[:, par, t, :, 0:D].rearrange("p (h c) d -> p c h d", c=KC), psum[:, 6, t * C:(t + 1) * C].rearrange("p (c h d) -> p c h d", c=KC, h=HP),
                                             bv_sb[:].rearrange("p (c h d) -> p c h d", c=KC, h=HP), ALU.add)
                last.then_inc(v_copied.sem, 1)

            def scale_rows(b, made, free, rs, summed, dst, scaled, banks):
                for t in range(NT):
                    heads = psum[:, banks[t], :].rearrange("p (h e) -> p h e", e=2 * D)
                    dve.wait_ge(made.sem, made.value(b, t + 1))
                    dve.reciprocal(rs[:, t, :], heads[:, :, D]).then_inc(summed.sem, 1)
                    dve.wait_ge(summed.sem, summed.value(b, t + 1))
                    if free is not None:
                        if begun(b - 1):
                            dve.wait_ge(free.sem, free.value(b - 1))
                    dve.tensor_tensor(dst[:, t, :].rearrange("p (c h d) -> p c h d", c=KC, h=HP),
                                      heads[:, :, 0:D].rearrange("p (h c) d -> p c h d", c=KC),
                                      rs[:, t, :].rearrange("p (h c) -> p c h", c=KC).unsqueeze(3).broadcast_to([P, KC, HP, D]), ALU.mult).then_inc(scaled.sem, 1)

            def stage_C(i, par):
                b, q = i - 1, 1 - par
                scale_rows(b, yt_made, None, rsum, rsum_made, y, y_scaled, (6, 7))
                dve.wait_ge(xres_loaded[q].sem, xres_loaded[q].value(b // 2))
                if begun(b - 2):
                    dve.wait_ge(x2_made.sem, x2_made.value(b - 2))
                for t in range(NT):
                    dve.wait_ge(y_scaled.sem, y_scaled.value(b, t + 1))
                    dve.tensor_tensor(x1[:, q, t, :], y[:, t, :], x_res[:, q, t, :], ALU.add).then_inc(x1_made.sem, 1)
                dve.wait_ge(x1_made.sem, x1_made.value(b))
                if begun(b - 1):
                    dve.wait_ge(czT_made.sem, czT_made.value(b - 1))
                layer_norm(b, x1[:, q], cz, cstats, cmv, ln2_step, crstd, ln2_rstd)

            def stage_D(i, par):
                b = i - 1
                dve.wait_ge(cq_high.sem, cq_high.value(b))
                if begun(b - 1):
                    dve.wait_ge(cq_low.sem, cq_low.value(b - 1))
                    dve.wait_ge(cq_mid.sem, cq_mid.value(b - 1))
                dve.tensor_tensor(cq_rest[:], cqT[:], cq_parts[:, 0, :], ALU.subtract).then_inc(cq_rest_made.sem, 1)

            def choose(i, par):
                b = i - 2
                dve.wait_ge(match_made.sem, match_made.value(b))
                dve.sem_inc(passed_dve, 1)
                for t in range(NT):
                    dve.max(top8[:, t, :], psum[:, 4, t * M:(t + 1) * M]).then_inc(match_step.sem, 1)
                for t in range(NT):
                    dve.wait_ge(match_step.sem, match_step.value(b, t + 1))
                    dve.sem_inc(passed_dve, 1)
                    dve.max_index(top8i[:, t, :], top8[:, t, :], psum[:, 4, t * M:(t + 1) * M]).then_inc(match_step.sem, 1)
                dve.wait_ge(match_step.sem, match_step.value(b, 2 * NT))
                dve.tensor_copy(first[:], top8i[:, :, 0]).then_inc(match_step.sem, 1)
                dve.wait_ge(match_step.sem, match_step.value(b))
                if begun(b - 1):
                    dve.wait_ge(count_made.sem, count_made.value(b - 1))
                for t in range(NT):
                    dve.tensor_scalar(onehot[:, t, :], iota_m, first[:, t:t + 1], None, ALU.is_equal).then_inc(onehot_made.sem, 1)

            def weigh(i, par):
                b = i - 2
                dve.wait_ge(count_made.sem, count_made.value(b))
                dve.tensor_copy(cnt_sb[0:M, :], psum[0:M, 5, 0:1]).then_inc(count_copied.sem, 1)
                if begun(b - 2):
                    dve.wait_ge(cst_made.sem, cst_made.value(b - 2))
                dve.tensor_scalar(KCx[KR:KR + 1, par, 0:M], psum[KR:KR + 1, 5, P:P + M], 0.0, NEG, ALU.is_equal, ALU.mult).then_inc(kmask_made.sem, 1)
                dve.wait_ge(count_copied.sem, count_copied.value(b))
                dve.wait_ge(ckv_copied.sem, ckv_copied.value(b))
                if begun(b - 2):
                    dve.wait_ge(cpv_made.sem, cpv_made.value(b - 2))
                dve.tensor_scalar(VC[0:M, par, 0:D], cv[0:M, :], cnt_sb[0:M, 0:1], None, ALU.mult).then_inc(vc_made.sem, 1)
                dve.tensor_copy(VC[0:M, par, D:D + 1], cnt_sb[0:M, :]).then_inc(vc_made.sem, 1)

            def residual_2(i, par):
                b, q = i - 3, 1 - par
                dve.wait_ge(o_made.sem, o_made.value(b))
                if begun(b - 2):
                    dve.wait_ge(rows_sent[q].sem, rows_sent[q].value((b - 2) // 2))
                dve.tensor_tensor(x2[:, q, :, 0:C], psum[:, 3, :].rearrange("p (t c) -> p t c", t=NT), x1[:, q], ALU.add).then_inc(x2_made.sem, 1)
                dve.tensor_scalar(x2[:, q, :, C], x2[:, q, :, C], 2.0 * T, None, ALU.add).then_inc(number_made.sem, 1)
                dve.wait_ge(x2_made.sem, x2_made.value(b))
                if begun(b - 1):
                    dve.wait_ge(rzT_made.sem, rzT_made.value(b - 1))
                layer_norm(b, x2[:, q, :, 0:C], rz, rstats, rmv, ln3_step, rrstd, ln3_rstd)

            def route(i, par):
                b = i - 4
                dve.wait_ge(logits_made.sem, logits_made.value(b))
                lg = psum[:, 7, 0:NT * E].rearrange("p (t e) -> p t e", t=NT)

                def spread(a):
                    return a[:].unsqueeze(2).broadcast_to([P, NT, E])
                dve.tensor_reduce(greatest[:], lg, AX_X, ALU.max).then_inc(route_step.sem, 1)
                dve.wait_ge(route_step.sem, route_step.value(b, 1))
                dve.tensor_tensor(equal[:], lg, spread(greatest), ALU.is_equal).then_inc(route_step.sem, 1)
                dve.wait_ge(route_step.sem, route_step.value(b, 2))
                dve.tensor_tensor(equal[:], equal[:], prefer.unsqueeze(1).broadcast_to([P, NT, E]), ALU.mult).then_inc(route_step.sem, 1)
                dve.wait_ge(route_step.sem, route_step.value(b, 3))
                dve.tensor_reduce(greatest[:], equal[:], AX_X, ALU.max).then_inc(route_step.sem, 1)
                dve.wait_ge(route_step.sem, route_step.value(b, 4))
                dve.tensor_tensor(chosen[:], equal[:], spread(greatest), ALU.is_equal).then_inc(route_step.sem, 1)
                if begun(b - 1):
                    dve.wait_ge(rank_made.sem, rank_made.value(b - 1))
                dve.wait_ge(route_step.sem, route_step.value(b, 5))
                dve.tensor_copy(chosen_bf[:], chosen[:]).then_inc(route_step.sem, 1)

            def find_rows(i, par):
                b = i - 4
                dve.wait_ge(rank_made.sem, rank_made.value(b))
                if begun(b - 1):
                    dve.wait_ge(place_step.sem, place_step.value(b - 1))
                dve.tensor_tensor(place[:], psum[:, 7, 0:NT * E].rearrange("p (t e) -> p t e", t=NT), next_row[:].unsqueeze(1).broadcast_to([P, NT, E]), ALU.add).then_inc(place_step.sem, 1)
                dve.wait_ge(place_step.sem, place_step.value(b, 1))
                dve.tensor_tensor(place[:], place[:], chosen[:], ALU.mult).then_inc(place_step.sem, 1)
                dve.wait_ge(place_step.sem, place_step.value(b, 2))
                dve.tensor_reduce(row_no[:], place[:], AX_X, ALU.add).then_inc(place_step.sem, 1)
                dve.wait_ge(place_step.sem, place_step.value(b, 3))
                if begun(b - 2):
                    dve.wait_ge(rows_sent[par].sem, rows_sent[par].value((b - 2) // 2))
                dve.tensor_copy(row_u[:, par, :], row_no[:]).then_inc(place_step.sem, 1)
                dve.tensor_tensor(next_row[:], psum[:, 7, NT * E:(NT + 1) * E], next_row[:], ALU.add).then_inc(place_step.sem, 1)

            def body(i, par):
                if runs(i, 0):
                    stage_A1(i, par)
                if runs(i, 2):
                    choose(i, par)
                if runs(i, 1):
                    stage_B(i, par)
                if runs(i, 2):
                    weigh(i, par)
                if runs(i, 3):
                    scale_rows(i - 3, cyt_made, cyC_made, crsum, crsum_made, cy, cy_scaled, (4, 5))
                if runs(i, 4):
                    route(i, par)
                if runs(i, 2):
                    stage_E(i, par)
                if runs(i, 3):
                    residual_2(i, par)
                if runs(i, 0):
                    stage_A2(i, par)
                if runs(i, 4):
                    find_rows(i, par)
                if runs(i, 0):
                    add_v_bias(i, par)
                if runs(i, 1):
                    stage_C(i, par)
                    stage_D(i, par)

            steps(dve, body)

            planned = [0]

            def plan(ins):
                ins.then_inc(plan_step, 1)
                planned[0] += 1
                dve.wait_ge(plan_step, planned[0])

            first_row = consts_sb[:, NEXT_ROW:NEXT_ROW + E]
            tile_nos = consts_sb[:, TILE_NOS:TILE_NOS + TILES]
            dve.wait_ge(place_step.sem, place_step.value(B - 1))
            plan(dve.tensor_tensor(count_f[:], next_row[:], first_row, ALU.subtract))
            plan(dve.tensor_scalar(count_i[:], count_f[:], float(TILE - 1), None, ALU.add))
            plan(dve.tensor_scalar(count_i[:], count_i[:], TILE.bit_length() - 1, None, ALU.logical_shift_right))
            plan(dve.tensor_copy(tiles_f[:], count_i[:]))
            plan(dve.tensor_scalar(jump[:], tiles_f[:], -float(TILE), float(ROOM), ALU.mult, ALU.add))
            for e in range(1, E):
                plan(dve.tensor_tensor(tiles_f[:, e:e + 1], tiles_f[:, e:e + 1], tiles_f[:, e - 1:e], ALU.add))
            plan(dve.tensor_scalar(tile_row[:], tile_nos, float(TILE), None, ALU.mult))
            for e in range(E):
                plan(dve.tensor_scalar(past[:, e, :], tile_nos, tiles_f[:, e:e + 1], None, ALU.is_ge))
                plan(dve.scalar_tensor_tensor(tile_row[:], past[:, e, :], jump[:, e:e + 1], tile_row[:], ALU.mult, ALU.add))
                if e:
                    plan(dve.tensor_tensor(tile_expert[:], tile_expert[:] if e > 1 else past[:, 0, :], past[:, e, :], ALU.add))
            plan(dve.tensor_scalar(tile_row_u[:], tile_row[:], float(E * ROOM), None, ALU.min))
            plan(dve.tensor_scalar(tile_expert_u[:], tile_expert[:], float(E - 1), None, ALU.min))
            plan(dve.tensor_copy(next_u[:], next_row[:]))
            assert planned[0] == PLAN_STEPS

            dve.wait_ge(pv_made.sem, pv_made.value(B - 1))
            dve.wait_ge(cst_made.sem, cst_made.value(B - 1))

            def prepare(k, par):
                dve.wait_ge(fx_loaded[par].sem, fx_loaded[par].value(k // 2))
                if begun(k - 1):
                    dve.wait_ge(fzT_made.sem, fzT_made.value(k - 1))
                    dve.wait_ge(zb_made.sem, zb_made.value(k - 1))
                layer_norm(k, fx[:, par, :, 0:C], fz, fstats, fmv, fln_step, frstd, fln_rstd, TS)
                if begun(k - 2):
                    dve.wait_ge(sent[par].sem, sent[par].value((k - 2) // 2))
                dve.tensor_copy(number_u[:, par, :], fx[:, par, :, C]).then_inc(numbers_made.sem, 1)

            def finish(k, par):
                b, q = k - 1, 1 - par
                dve.wait_ge(zb_made.sem, zb_made.value(b))
                if begun(b - 1):
                    dve.wait_ge(final_made.sem, final_made.value(b - 1))
                for half in range(2):
                    dve.wait_ge(ffn_made.sem, ffn_made.value(b, half + 1))
                    dve.tensor_tensor(ysum[:, 2 * half:2 * half + 2, :], psum[:, 4 + half, :].rearrange("p (j c) -> p j c", j=2), zb[:, q, 2 * half:2 * half + 2, :], ALU.add).then_inc(ysum_made.sem, 1)
                for j in range(TS):
                    dve.wait_ge(ysum_made.sem, ysum_made.value(b, j // 2 + 1))
                    dve.bn_stats(ostats[:, j, :], ysum[:, j, :]).then_inc(oln_step.sem, 1)
                for j in range(TS):
                    dve.wait_ge(oln_step.sem, oln_step.value(b, j + 1))
                    dve.sem_inc(passed_dve, 1)
                    dve.bn_aggr(omv[:, j, :], ostats[:, j, :]).then_inc(oln_step.sem, 1)
                for j in range(TS):
                    dve.wait_ge(oln_step.sem, oln_step.value(b, TS + j + 1))
                    dve.scalar_tensor_tensor(ysum[:, j, :], ysum[:, j, :], omv[:, j, 0:1], gamma_sb[:], ALU.subtract, ALU.mult).then_inc(oln_step.sem, 1)
                dve.wait_ge(oln_rstd.sem, oln_rstd.value(b))
                dve.wait_ge(xb_made.sem, xb_made.value(b))
                if begun(b - 2):
                    dve.wait_ge(sent[q].sem, sent[q].value((b - 2) // 2))
                for j in range(TS):
                    dve.wait_ge(oln_step.sem, oln_step.value(b, 2 * TS + j + 1))
                    dve.scalar_tensor_tensor(final[:, q, j, :], ysum[:, j, :], orstd[:, j:j + 1], xb[:, q, j, :], ALU.mult, ALU.add).then_inc(final_made.sem, 1)

            def tile_body(k, par):
                if tile_runs(k, 0):
                    prepare(k, par)
                if tile_runs(k, 1):
                    finish(k, par)

            tile_steps(dve, tile_body)

        @block.gpsimd
        def _(pool):
            def root(b, step, mean_var, rs, made, eps, NT=NT):
                pool.wait_ge(step.sem, step.value(b, 2 * NT))
                pool.sem_inc(passed_pool, 1)
                pool.tensor_scalar(rs[:], mean_var[:, :, 1], eps, None, ALU.add).then_inc(made.sem, 1)
                pool.wait_ge(made.sem, made.value(b, 1))
                pool.sem_inc(passed_pool, 1)
                pool.tensor_tensor(rs[:], rs[:], minus_half[:, 0:NT], ALU.pow).then_inc(made.sem, 1)

            def send_rows(i, par):
                b = i - 4
                pool.wait_ge(place_step.sem, place_step.value(b))
                pool.sem_inc(passed_pool, 1)
                pool.wait_ge(x2_made.sem, x2_made.value(b))
                pool.sem_inc(passed_pool, 1)
                pool.wait_ge(number_made.sem, number_made.value(b))
                pool.sem_inc(passed_pool, 1)
                for t in range(NT):
                    pool.indirect_dma_start(out=rows_dram, out_offset=bass.IndirectOffsetOnAxis(ap=row_u[:, par, t:t + 1], axis=0),
                                            in_=x2[:, par, t, :], in_offset=None).then_inc(rows_sent[par].sem, 16)

            def split_k(i, par):
                b, q = i - 1, 1 - par
                R = slice(0, KR)
                pool.wait_ge(ckv_copied.sem, ckv_copied.value(b, 1))
                pool.sem_inc(passed_pool, 1)
                chain = [
                    lambda: pool.tensor_copy(kc_h[R], kc32[R]),
                    lambda: pool.tensor_tensor(kc_r[R], kc32[R], kc_h[R], ALU.subtract),
                    lambda: pool.tensor_copy(kc_m[R], kc_r[R]),
                    lambda: pool.tensor_tensor(kc_r2[R], kc_r[R], kc_m[R], ALU.subtract),
                    lambda: pool.tensor_scalar(kc_a[R], kc_h[R], part_mask[R, 0:1], None, ALU.mult),
                    lambda: pool.tensor_scalar(kc_b[R], kc_m[R], part_mask[R, 1:2], None, ALU.mult),
                    lambda: pool.tensor_tensor(kc_a[R], kc_a[R], kc_b[R], ALU.add),
                    lambda: pool.tensor_scalar(kc_b[R], kc_r2[R], part_mask[R, 2:3], None, ALU.mult),
                    lambda: pool.tensor_tensor(KCx[R, q, 0:M], kc_a[R], kc_b[R], ALU.add),
                ]
                if begun(b - 2):
                    pool.wait_ge(cst_made.sem, cst_made.value(b - 2))
                    pool.sem_inc(passed_pool, 1)
                for k, op in enumerate(chain):
                    if k:
                        pool.wait_ge(kc_step.sem, kc_step.value(b, k))
                        pool.sem_inc(passed_pool, 1)
                    op().then_inc(kc_step.sem, 1)

            def body(i, par):
                if runs(i, 0):
                    root(i, ln1_step, mv, rstd, ln1_rstd, LN_EPS)
                if runs(i, 3):
                    root(i - 3, ln3_step, rmv, rrstd, ln3_rstd, LN_EPS)
                if runs(i, 0):
                    pool.wait_ge(q_mid.sem, q_mid.value(i))
                    pool.sem_inc(passed_pool, 1)
                    pool.tensor_tensor(q_parts[:, 2, :], q_rest[:], q_parts[:, 1, :], ALU.subtract).then_inc(q_low.sem, 1)
                    pool.wait_ge(k_mid.sem, k_mid.value(i))
                    pool.sem_inc(passed_pool, 1)
                    pool.tensor_tensor(k_parts[:, 2, :], k_rest[:], k_parts[:, 1, :], ALU.subtract).then_inc(k_low.sem, 1)
                if runs(i, 4):
                    send_rows(i, par)
                if runs(i, 1):
                    split_k(i, par)
                    root(i - 1, ln2_step, cmv, crstd, ln2_rstd, LN_EPS)
                    if begun(i - 1):
                        pool.wait_ge(cq_mid.sem, cq_mid.value(i - 1))
                        pool.sem_inc(passed_pool, 1)
                    pool.tensor_tensor(cq_parts[:, 2, :], cq_rest[:], cq_parts[:, 1, :], ALU.subtract).then_inc(cq_low.sem, 1)

            pool.wait_ge(consts_ready, CONSTS)
            pool.memset(padding[:, :, 0:C], 0.0).then_inc(padding_made, 1)
            pool.memset(padding[:, :, C:ROW], float(B * T)).then_inc(padding_made, 1)
            steps(pool, body)

            pool.wait_ge(st_made.sem, st_made.value(B - 1))
            pool.sem_inc(passed_pool, 1)

            def tile_body(k, par):
                if tile_runs(k, 0):
                    root(k, fln_step, fmv, frstd, fln_rstd, LN_EPS, TS)
                    if begun(k - 2):
                        pool.wait_ge(ysum_made.sem, ysum_made.value(k - 2))
                        pool.sem_inc(passed_pool, 1)
                    pool.wait_ge(fln_step.sem, fln_step.value(k))
                    pool.sem_inc(passed_pool, 1)
                    pool.tensor_tensor(zb[:, par], fz[:], bo_sb[:].unsqueeze(1).broadcast_to([P, TS, C]), ALU.add).then_inc(zb_made.sem, 1)
                    if begun(k - 2):
                        pool.wait_ge(final_made.sem, final_made.value(k - 2))
                        pool.sem_inc(passed_pool, 1)
                    pool.wait_ge(fx_loaded[par].sem, fx_loaded[par].value(k // 2))
                    pool.sem_inc(passed_pool, 1)
                    pool.tensor_tensor(xb[:, par], fx[:, par, :, 0:C], beta_sb[:].unsqueeze(1).broadcast_to([P, TS, C]), ALU.add).then_inc(xb_made.sem, 1)
                if tile_runs(k, 1):
                    b, q = k - 1, 1 - par
                    root(b, oln_step, omv, orstd, oln_rstd, OUT_LN_EPS, TS)
                    pool.wait_ge(numbers_made.sem, numbers_made.value(b))
                    pool.sem_inc(passed_pool, 1)
                    for j in range(TS):
                        pool.wait_ge(final_made.sem, final_made.value(b, j + 1))
                        pool.sem_inc(passed_pool, 1)
                        pool.indirect_dma_start(out=out.rearrange("b t c -> (b t) c"), out_offset=bass.IndirectOffsetOnAxis(ap=number_u[:, q, j:j + 1], axis=0),
                                                in_=final[:, q, j, :], in_offset=None, bounds_check=B * T - 1, oob_is_err=False).then_inc(sent[q].sem, 16)

            tile_steps(pool, tile_body)
            for k in (TILES - 2, TILES - 1):
                pool.wait_ge(sent[k % 2].sem, sent[k % 2].value(k // 2))
                pool.sem_inc(passed_pool, 1)


def kernel(**inputs):
    import numpy as np
    import concourse.bacc as bacc
    from concourse.bass_utils import run_bass_kernel_spmd

    arrays = layout(inputs)
    nc = bacc.Bacc("TRN2", target_bir_lowering=False, num_devices=1)
    args = [nc.dram_tensor(f"in_{name}", a.shape, mybir.dt.from_np(a.dtype), kind="ExternalInput").ap() for name, a in arrays.items()]
    shape = inputs["x"].shape
    args.append(nc.dram_tensor("out_dram", shape, F32, kind="ExternalOutput").ap())
    decoder_kernel(nc, *args)
    result = run_bass_kernel_spmd(nc, [{f"in_{name}": a for name, a in arrays.items()}], core_ids=[0])
    return result.results[0]["out_dram"]


def layout(inputs):
    import numpy as np

    def c(a):
        return np.ascontiguousarray(a)

    i = {k: np.asarray(v) for k, v in inputs.items()}
    row, col = np.arange(P)[:, None], np.arange(P)[None, :]
    tiles = i["x"].shape[0] * T // TILE + E - 1
    consts = np.zeros((P, TILE_NOS + tiles), np.float32)
    consts[:, TILE_NOS:] = np.arange(tiles)
    consts[:, 0:P] = np.eye(P)
    consts[:, P:2 * P] = np.where(col > row, NEG, 0.0)
    consts[:, 2 * P:3 * P] = np.where(row > col, NEG, 0.0)
    consts[:, 3 * P:3 * P + M] = np.arange(M)
    for t, part in enumerate(K_PARTS):
        consts[D * t:D * t + D, 3 * P + M + part] = 1.0
    tokens = i["x"].shape[0] * T
    consts[:, BEFORE - E:BEFORE] = E - np.arange(E)
    consts[:, BEFORE:BEFORE + P] = row < col
    consts[:, NEXT_ROW:NEXT_ROW + E] = np.arange(E) * (tokens + TILE)
    consts[:, NUMBERS:TILE_NOS] = row + P * np.arange(2 * NT)[None, :] - 2 * T
    return {
        "x": c(i["x"]),
        "ctxT": c(i["ctx_1024"].transpose(0, 2, 1)),
        "wqkvT": c(i["L0_attn_W"].T),
        "bqkT": c(i["L0_attn_b"][:2 * C].reshape(2 * KC, P).T),
        "bv": c(i["L0_attn_b"][2 * C:].reshape(1, C)),
        "wqT": c(i["L0_xattn_Wq"].T),
        "wkvT": c(i["L0_xattn_Wkv"].T),
        "wcT": c(i["L0_xattn_Wc"].T),
        "w_router": c(i["L0_ffn_W_router"]),
        "w1": c(i["L0_ffn_W1"]),
        "b1T": c(i["L0_ffn_b1"].reshape(E, MI, P).transpose(0, 2, 1)),
        "wo": c(i["L0_ffn_Wo"]),
        "bo": c(i["L0_ffn_bo"].reshape(1, C)),
        "gamma": c(i["L0_ffn_ln_gamma"].reshape(1, C)),
        "beta": c(i["L0_ffn_ln_beta"].reshape(1, C)),
        "consts": consts,
    }
```

```python
from contextlib import ExitStack

import concourse.bass as bass
from concourse import mybir
from concourse.alu_op_type import AluOpType as ALU

F32 = mybir.dt.float32
F32R = mybir.dt.float32r
BF16 = mybir.dt.bfloat16
U32 = mybir.dt.uint32
I32 = mybir.dt.int32
ACT = mybir.ActivationFunctionType
AX_X = mybir.AxisListType.X

P = 128
C = 256
KC = C // P
T = 256
NT = T // P
H = 16
D = C // H
HP = H // KC
M = 120
E = 4
I = 1024
NTERM = 6
KR = NTERM * D
NEG = -1e30
LN_EPS = 1e-5
LAGS = 4
TILE = 512
TS = TILE // P
MI = I // P
ROW = C + 1
OUT_LN_EPS = 1e-12
H_LOW_POOL = (5, 7)
H_LOW_DVE = tuple(m for m in range(MI) if m not in H_LOW_POOL)
Q_PARTS = (0, 0, 0, 1, 1, 2)
K_PARTS = (0, 1, 2, 0, 1, 0)


BEFORE = 3 * P + M + 3 + E
NEXT_ROW = BEFORE + P
NUMBERS = NEXT_ROW + E
TILE_NOS = NUMBERS + 2 * NT


class Signal:

    def __init__(self, sem, per_sequence):
        self.sem = sem
        self.per_sequence = per_sequence

    def value(self, b, k=None):
        return b * self.per_sequence + (self.per_sequence if k is None else k)


def begun(b):
    return not isinstance(b, int) or b >= 0


def decoder_kernel(nc, x, ctxT, wqkvT, bqkT, bv, wqT, wkvT, wcT, w_router, w1, b1T, wo, bo, gamma, beta, consts, out):
    B = x.shape[0]
    assert B % 2 == 0 and B >= 8

    with ExitStack() as stack:
        def sb(name, shape, dt=F32):
            return stack.enter_context(nc.sbuf_tensor(name, shape, dt))

        def signal(name, per_sequence, step=1):
            return Signal(stack.enter_context(nc.semaphore(name)), per_sequence * step)

        def dma_signal(name, per_sequence):
            return [Signal(stack.enter_context(nc.semaphore(f"{name}{par}")), 16 * per_sequence) for par in range(2)]

        def semaphore(name):
            return stack.enter_context(nc.semaphore(name))

        psum = stack.enter_context(nc.psum_tensor("psum", [P, 8, 512], F32))
        S_BANKS, ST_BANKS, Y_BANKS, MISC_BANKS = (0, 1), (2, 3), (4, 5), (6, 7)

        parts_dram = {
            name: nc.dram_tensor(f"parts_{name}", (2, 3, HP, D, KC * T), BF16).ap() for name in ("q", "k", "qc")
        }

        ROOM = B * T + TILE
        rows_dram = nc.dram_tensor("rows_dram", (E * ROOM + TILE, ROW), F32).ap()

        ident_bf = sb("ident_bf", [P, P], BF16)
        ones_bf = sb("ones_bf", [P, P], BF16)
        mask_s = sb("mask_s", [P, P], BF16)
        mask_t = sb("mask_t", [P, P], BF16)
        consts_sb = sb("consts_sb", [P, TILE_NOS + B * T // TILE + E - 1])
        iota_m = consts_sb[:, 3 * P:3 * P + M]
        part_mask = consts_sb[:, 3 * P + M:3 * P + M + 3]
        ident = consts_sb[:, 0:P]
        minus_half = sb("minus_half", [P, TS])
        wqkv_sb = sb("wqkv_sb", [P, KC, 3 * C])
        bqk_sb = sb("bqk_sb", [P, 2 * KC])
        bv_sb = sb("bv_sb", [P, C])
        wq_sb = sb("wq_sb", [P, KC, C])
        wmk_sb = sb("wmk_sb", [P, KC, KR])
        wmv_sb = sb("wmv_sb", [P, KC, D])
        wc_sb = sb("wc_sb", [P, KC, C])

        TILES = B * T // TILE + E - 1
        next_row = sb("next_row", [P, E])
        b1_sb = sb("b1_sb", [P, 2, MI])
        wo_sb = sb("wo_sb", [P, MI, C])
        bo_sb = sb("bo_sb", [P, C])
        gamma_sb = sb("gamma_sb", [P, C])
        beta_sb = sb("beta_sb", [P, C])
        padding = sb("padding", [P, TS, ROW])
        count_f = sb("count_f", [P, E])
        count_i = sb("count_i", [P, E], I32)
        tiles_f = sb("tiles_f", [P, E])
        jump = sb("jump", [P, E])
        past = sb("past", [P, E, TILES])
        tile_row = sb("tile_row", [P, TILES])
        tile_expert = sb("tile_expert", [P, TILES])
        next_u = sb("next_u", [P, E], U32)
        tile_row_u = sb("tile_row_u", [P, TILES + 1], U32)
        tile_expert_u = sb("tile_expert_u", [P, TILES + 1], U32)

        attention_stack = ExitStack()

        def during_attention(name, shape, dt=F32):
            return attention_stack.enter_context(nc.sbuf_tensor(name, shape, dt))

        x_in = during_attention("x_in", [P, 2, NT, C])
        x_res = during_attention("x_res", [P, 2, NT, C])
        ctx_sb = during_attention("ctx_sb", [P, 2, KC, M])
        stats = during_attention("stats", [P, NT, 6])
        mv = during_attention("mv", [P, NT, 2])
        rstd = during_attention("rstd", [P, NT])
        z = during_attention("z", [P, NT, C])
        zT = during_attention("zT", [P, KC, T])
        q_parts = during_attention("q_parts", [P, 3, KC * T], BF16)
        q_rest = during_attention("q_rest", [P, KC * T])
        k_parts = during_attention("k_parts", [P, 3, KC * T], BF16)
        k_rest = during_attention("k_rest", [P, KC * T])
        QP = during_attention("QP", [P, 2, H, T], BF16)
        KP = during_attention("KP", [P, 2, H, T], BF16)
        V = during_attention("V", [P, 2, NT, H, 2 * D])
        negmax = during_attention("negmax", [P, NT, H])
        mx2 = during_attention("mx2", [P, NT, 2, H], BF16)
        mxT = during_attention("mxT", [2 * H, T], BF16)
        PA = during_attention("PA", [P, H, T])
        PB = during_attention("PB", [P, H, P])
        yT = during_attention("yT", [P, H // 4, T])
        rsum = during_attention("rsum", [P, NT, H])
        y = during_attention("y", [P, NT, C])
        x1 = during_attention("x1", [P, 2, NT, C])
        cz = during_attention("cz", [P, NT, C])
        czT = during_attention("czT", [P, KC, T])
        cstats = during_attention("cstats", [P, NT, 6])
        cmv = during_attention("cmv", [P, NT, 2])
        crstd = during_attention("crstd", [P, NT])
        cqT = during_attention("cqT", [P, KC * T])
        cq_parts = during_attention("cq_parts", [P, 3, KC * T], BF16)
        cq_rest = during_attention("cq_rest", [P, KC * T])
        QC = during_attention("QC", [P, 2, H, T], BF16)
        KCx = during_attention("KCx", [P, 2, P], BF16)
        kc32 = during_attention("kc32", [P, M])
        kc_h = during_attention("kc_h", [P, M], BF16)
        kc_m = during_attention("kc_m", [P, M], BF16)
        kc_r = during_attention("kc_r", [P, M])
        kc_r2 = during_attention("kc_r2", [P, M])
        kc_a = during_attention("kc_a", [P, M])
        kc_b = during_attention("kc_b", [P, M])
        cv = during_attention("cv", [P, 2, D])
        VC = during_attention("VC", [P, 2, 2 * D])
        cnt_sb = during_attention("cnt_sb", [P, 1])
        top8 = during_attention("top8", [P, NT, 8])
        top8i = during_attention("top8i", [P, NT, 8], U32)
        first = during_attention("first", [P, NT])
        onehot = during_attention("onehot", [P, NT, M], BF16)
        cnegmax = during_attention("cnegmax", [P, NT, H])
        cmx2 = during_attention("cmx2", [P, NT, 2, H], BF16)
        cmxT = during_attention("cmxT", [2 * H, T], BF16)
        PC = during_attention("PC", [P, H, T])
        cyT = during_attention("cyT", [P, H // 4, T])
        crsum = during_attention("crsum", [P, NT, H])
        cy = during_attention("cy", [P, NT, C])
        cyC = during_attention("cyC", [P, KC, T])
        x2 = during_attention("x2", [P, 2, NT, ROW])
        rz = during_attention("rz", [P, NT, C])
        rzT = during_attention("rzT", [P, KC, T])
        rstats = during_attention("rstats", [P, NT, 6])
        rmv = during_attention("rmv", [P, NT, 2])
        rrstd = during_attention("rrstd", [P, NT])
        wr_sb = during_attention("wr_sb", [P, KC, E])
        before_bf = during_attention("before_bf", [P, P], BF16)
        prefer = consts_sb[:, 3 * P + M + 3:3 * P + M + 3 + E]
        greatest = during_attention("greatest", [P, NT])
        equal = during_attention("equal", [P, NT, E])
        chosen = during_attention("chosen", [P, NT, E])
        chosen_bf = during_attention("chosen_bf", [P, NT, E], BF16)
        place = during_attention("place", [P, NT, E])
        row_no = during_attention("row_no", [P, NT])
        row_u = during_attention("row_u", [P, 2, NT], U32)

        attention_stack.close()

        w1_sb = sb("w1_sb", [P, 2, KC, I])
        fzT = sb("fzT", [P, KC, TILE])
        hT = sb("hT", [P, MI, TILE])
        w1_high = sb("w1_high", [P, 2, KC, I], F32R)
        w1_low = sb("w1_low", [P, 2, KC, I], F32R)
        wo_high = sb("wo_high", [P, MI, C], F32R)
        wo_low = sb("wo_low", [P, MI, C], F32R)
        fzT_high = sb("fzT_high", [P, KC, TILE], F32R)
        fzT_low = sb("fzT_low", [P, KC, TILE], F32R)
        hT_high = sb("hT_high", [P, MI, TILE], F32R)
        hT_low = sb("hT_low", [P, MI, TILE], F32R)
        fz = sb("fz", [P, TS, C])
        zb = sb("zb", [P, 2, TS, C])
        xb = sb("xb", [P, 2, TS, C])
        ysum = sb("ysum", [P, TS, C])
        final = sb("final", [P, 2, TS, C])
        fx = sb("fx", [P, 2, TS, ROW])
        fstats = sb("fstats", [P, TS, 6])
        fmv = sb("fmv", [P, TS, 2])
        frstd = sb("frstd", [P, TS])
        ostats = sb("ostats", [P, TS, 6])
        omv = sb("omv", [P, TS, 2])
        orstd = sb("orstd", [P, TS])
        number_f = sb("number_f", [P, 2, TS])
        number_u = sb("number_u", [P, 2, TS], U32)

        PLAN_STEPS = 5 + (E - 1) + 1 + 2 * E + (E - 1) + 3
        plan_step = semaphore("plan_step")
        padding_made = semaphore("padding_made")
        padded = semaphore("padded")
        fx_loaded = dma_signal("fx_loaded", 1)
        w1_loaded = dma_signal("w1_loaded", 2)
        sent = dma_signal("sent", TS)
        fln_step = signal("fln_step", 3 * TS)
        fln_rstd = signal("fln_rstd", 2)
        fzT_made = signal("fzT_made", KC)
        fzT_copied = signal("fzT_copied", KC)
        h_made = signal("h_made", MI)
        gelu_done = signal("gelu_done", MI)
        ffn_made = signal("ffn_made", 2)
        zb_made = signal("zb_made", 1)
        xb_made = signal("xb_made", 1)
        number_kept = signal("number_kept", 1)
        numbers_made = signal("numbers_made", 1)
        z_high_made = signal("z_high_made", KC)
        z_low_made = signal("z_low_made", KC)
        w1_high_made = signal("w1_high_made", KC)
        w1_low_made = signal("w1_low_made", KC)
        h_high_made = signal("h_high_made", MI)
        h_low_dve = signal("h_low_dve", len(H_LOW_DVE))
        h_low_pool = signal("h_low_pool", len(H_LOW_POOL))
        wo_split = semaphore("wo_split")
        ysum_made = signal("ysum_made", 2)
        oln_step = signal("oln_step", 3 * TS)
        oln_rstd = signal("oln_rstd", 2)
        final_made = signal("final_made", TS)
        rows_sent = dma_signal("rows_sent", NT)
        rzT_made = signal("rzT_made", 1)
        rzT_copied = signal("rzT_copied", 1)
        logits_made = signal("logits_made", 1)
        rank_made = signal("rank_made", 1)
        ln3_step = signal("ln3_step", 3 * NT)
        ln3_rstd = signal("ln3_rstd", 2)
        route_step = signal("route_step", 6)
        number_made = signal("number_made", 1)
        place_step = signal("place_step", 5)
        consts_in = semaphore("consts_in")
        consts_ready = semaphore("consts_ready")
        VECTOR_CONSTS = 9
        gpsimd_consts = semaphore("gpsimd_consts")
        GPSIMD_CONSTS = 7
        N_FIRST_LOADS = 3
        first_weights_in = semaphore("first_weights_in")
        N_WEIGHT_LOADS = 8 + NTERM
        weights_in = semaphore("weights_in")
        x_loaded = dma_signal("x_loaded", 1)
        xres_loaded = dma_signal("xres_loaded", 1)
        ctx_loaded = dma_signal("ctx_loaded", 1)
        q_stored = dma_signal("q_stored", 1)
        k_stored = dma_signal("k_stored", 1)
        q_packed = dma_signal("q_packed", NTERM)
        k_packed = dma_signal("k_packed", NTERM)
        mx_packed = dma_signal("mx_packed", 2)
        cq_stored = dma_signal("cq_stored", 1)
        cq_packed = dma_signal("cq_packed", NTERM)
        cmx_packed = dma_signal("cmx_packed", 2)
        xT_made = signal("xT_made", 1)
        q_made = signal("q_made", 1)
        k_made = signal("k_made", 1)
        v_made = signal("v_made", 1)
        s_made = signal("s_made", 12)
        mxT_made = signal("mxT_made", 1)
        st_made = signal("st_made", 12)
        pv_made = signal("pv_made", 2)
        yt_made = signal("yt_made", 2)
        czT_made = signal("czT_made", 1)
        cq_made = signal("cq_made", 1)
        ckv_made = signal("ckv_made", 1)
        match_made = signal("match_made", 1)
        count_made = signal("count_made", 1)
        cs_made = signal("cs_made", 8)
        cmxT_made = signal("cmxT_made", 1)
        cst_made = signal("cst_made", 8)
        cpv_made = signal("cpv_made", 2)
        cyt_made = signal("cyt_made", 2)
        cyC_made = signal("cyC_made", 1)
        o_made = signal("o_made", 1)
        zT_copied = signal("zT_copied", 1)
        q_high = signal("q_high", 1)
        k_high = signal("k_high", 1)
        q_mid = signal("q_mid", 1)
        k_mid = signal("k_mid", 1)
        exp_done = signal("exp_done", 12)
        mxT_copied = signal("mxT_copied", 1)
        yT_copied = signal("yT_copied", 2)
        czT_copied = signal("czT_copied", 1)
        cq_copied = signal("cq_copied", 1)
        cq_high = signal("cq_high", 1)
        cq_mid = signal("cq_mid", 1)
        ckv_copied = signal("ckv_copied", 2)
        cexp_done = signal("cexp_done", 8)
        cmxT_copied = signal("cmxT_copied", 1)
        cyT_copied = signal("cyT_copied", 2)
        cyC_copied = signal("cyC_copied", 1)
        LN_STEPS = 2 * NT + NT
        ln1_step = signal("ln1_step", LN_STEPS)
        q_rest_made = signal("q_rest_made", 1)
        k_rest_made = signal("k_rest_made", 1)
        v_copied = signal("v_copied", 1)
        max_done = signal("max_done", 12)
        mx_split = signal("mx_split", 2)
        rsum_made = signal("rsum_made", 2)
        y_scaled = signal("y_scaled", 2)
        x1_made = signal("x1_made", 2)
        ln2_step = signal("ln2_step", LN_STEPS)
        cq_rest_made = signal("cq_rest_made", 1)
        match_step = signal("match_step", 2 * NT + 1)
        onehot_made = signal("onehot_made", NT)
        count_copied = signal("count_copied", 1)
        kmask_made = signal("kmask_made", 1)
        vc_made = signal("vc_made", 2)
        cmax_done = signal("cmax_done", 8)
        cmx_split = signal("cmx_split", 2)
        crsum_made = signal("crsum_made", 2)
        cy_scaled = signal("cy_scaled", 2)
        x2_made = signal("x2_made", 1)
        ln1_rstd = signal("ln1_rstd", 2)
        ln2_rstd = signal("ln2_rstd", 2)
        q_low = signal("q_low", 1)
        k_low = signal("k_low", 1)
        cq_low = signal("cq_low", 1)
        kc_step = signal("kc_step", 9)

        passed_sp = semaphore("passed_sp")
        passed_pool = semaphore("passed_pool")
        passed_dve = semaphore("passed_dve")
        passed_act = semaphore("passed_act")

        def steps(eng, body):
            for i in range(6):
                body(i, i % 2)
            with eng.Fori(6, B, 2) as i:
                body(i, 0)
                body(i + 1, 1)
            for i in range(B, B + LAGS):
                body(i, i % 2)

        def runs(i, lag):
            return not isinstance(i, int) or 0 <= i - lag < B

        def tile_steps(eng, body):
            for k in range(4):
                body(k, k % 2)
            end = TILES - 1 - (TILES - 1) % 2
            with eng.Fori(4, end, 2) as k:
                body(k, 0)
                body(k + 1, 1)
            for k in range(end, TILES + 2):
                body(k, k % 2)

        def tile_runs(k, lag):
            return not isinstance(k, int) or 0 <= k - lag < TILES

        block = stack.enter_context(nc.Block())

        @block.sync
        def _(sp):
            sp.dma_start(consts_sb[:], consts).then_inc(consts_in, 16)
            setup = [
                (wqkv_sb[:], wqkvT.rearrange("(c p) n -> p c n", p=P)),
                (bqk_sb[:], bqkT),
                (bv_sb[:], bv.broadcast_to([P, C])),
                (wq_sb[:], wqT.rearrange("(c p) n -> p c n", p=P)),
                (wc_sb[:], wcT.rearrange("(c p) n -> p c n", p=P)),
                (wo_sb[:], wo.rearrange("(m p) n -> p m n", p=P)),
                (bo_sb[:], bo.broadcast_to([P, C])),
                (gamma_sb[:], gamma.broadcast_to([P, C])),
                (beta_sb[:], beta.broadcast_to([P, C])),
                (wr_sb[:], w_router.rearrange("(c p) n -> p c n", p=P)),
                (wmv_sb[:], wkvT[:, D:2 * D].rearrange("(c p) n -> p c n", p=P)),
            ] + [(wmk_sb[:, :, D * t:D * t + D], wkvT[:, 0:D].rearrange("(c p) n -> p c n", p=P)) for t in range(NTERM)]
            assert len(setup) == N_FIRST_LOADS + N_WEIGHT_LOADS

            def load_x(b, par):
                if begun(b - 2):
                    sp.wait_ge(ln1_step.sem, ln1_step.value(b - 2))
                    sp.sem_inc(passed_sp, 1)
                sp.dma_start(x_in[:, par], x[bass.ds(b % B, 1)].rearrange("o (t p) c -> p (o t) c", p=P)).then_inc(x_loaded[par].sem, 16)

            def store_parts(b, par, name, parts, low, stored):
                sp.wait_ge(low.sem, low.value(b))
                sp.sem_inc(passed_sp, 1)
                sp.dma_start(parts_dram[name][par].rearrange("y h d n -> (h d) y n"), parts[:]).then_inc(stored[par].sem, 16)

            def pack(b, par, name, stored, packed, dst, reader):
                sp.wait_ge(stored[par].sem, stored[par].value(b // 2))
                sp.sem_inc(passed_sp, 1)
                if begun(b - 2):
                    sp.wait_ge(reader.sem, reader.value(b - 2))
                    sp.sem_inc(passed_sp, 1)
                for t, part in enumerate(K_PARTS if name == "k" else Q_PARTS):
                    sp.dma_start(dst[D * t:D * t + D, par].rearrange("d (h c) n -> d h (c n)", h=HP),
                                 parts_dram[name][par, part].rearrange("h d n -> d h n")).then_inc(packed[par].sem, 16)

            def body(i, par):
                if runs(i, 0):
                    load_x(i + 2, par)
                if runs(i, 1):
                    if begun(i - 3):
                        sp.wait_ge(x1_made.sem, x1_made.value(i - 3))
                        sp.sem_inc(passed_sp, 1)
                    sp.dma_start(x_res[:, 1 - par], x[bass.ds(i - 1, 1)].rearrange("o (t p) c -> p (o t) c", p=P)).then_inc(xres_loaded[1 - par].sem, 16)
                    if begun(i - 3):
                        sp.wait_ge(match_made.sem, match_made.value(i - 3))
                        sp.sem_inc(passed_sp, 1)
                    sp.dma_start(ctx_sb[:, 1 - par], ctxT[bass.ds(i - 1, 1)].rearrange("o (c p) m -> p (o c) m", p=P)).then_inc(ctx_loaded[1 - par].sem, 16)
                if runs(i, 0):
                    store_parts(i, par, "q", q_parts, q_low, q_stored)
                    store_parts(i, par, "k", k_parts, k_low, k_stored)
                    pack(i, par, "q", q_stored, q_packed, QP, st_made)
                    pack(i, par, "k", k_stored, k_packed, KP, st_made)
                if runs(i, 2):
                    store_parts(i - 2, par, "qc", cq_parts, cq_low, cq_stored)
                    pack(i - 2, par, "qc", cq_stored, cq_packed, QC, cst_made)
                    sp.wait_ge(cmxT_copied.sem, cmxT_copied.value(i - 2))
                    sp.sem_inc(passed_sp, 1)
                    for part in range(2):
                        sp.dma_start(QC[KR + 1 + part:KR + 2 + part, par], cmxT[H * part:H * part + H, :]).then_inc(cmx_packed[par].sem, 16)

            load_x(0, 0)
            for n, (dst, src) in enumerate(setup):
                if n < N_FIRST_LOADS:
                    sp.dma_start(dst, src).then_inc(first_weights_in, 16)
                else:
                    sp.dma_start(dst, src).then_inc(weights_in, 16)
                if n == N_FIRST_LOADS - 1:
                    load_x(1, 1)
            steps(sp, body)

            sp.wait_ge(rank_made.sem, rank_made.value(B - 1))
            sp.wait_ge(rzT_copied.sem, rzT_copied.value(B - 1))
            sp.wait_ge(place_step.sem, place_step.value(B - 1))
            sp.wait_ge(kc_step.sem, kc_step.value(B - 1))
            sp.wait_ge(ln3_rstd.sem, ln3_rstd.value(B - 1))
            for par in range(2):
                sp.wait_ge(x_loaded[par].sem, x_loaded[par].value(B // 2))
                sp.wait_ge(rows_sent[par].sem, rows_sent[par].value(B // 2 - 1))
            sp.wait_ge(plan_step, PLAN_STEPS)
            sp.wait_ge(padding_made, 2)
            for e in range(E):
                start = sp.value_load(next_u[0:1, e:e + 1], min_val=e * ROOM, max_val=e * ROOM + B * T)
                sp.dma_start(rows_dram[bass.ds(start, TILE)].rearrange("(p j) c -> p (j c)", p=P), padding[:].rearrange("p j c -> p (j c)")).then_inc(padded, 16)
            sp.dma_start(rows_dram[E * ROOM:E * ROOM + TILE].rearrange("(p j) c -> p (j c)", p=P), padding[:].rearrange("p j c -> p (j c)")).then_inc(padded, 16)

            def load_rows(k, par):
                row = sp.value_load(tile_row_u[0:1, bass.ds(k, 1)], min_val=0, max_val=E * ROOM)
                if begun(k - 2):
                    sp.wait_ge(fln_step.sem, fln_step.value(k - 2))
                    sp.sem_inc(passed_sp, 1)
                    sp.wait_ge(xb_made.sem, xb_made.value(k - 2))
                    sp.sem_inc(passed_sp, 1)
                    sp.wait_ge(number_kept.sem, number_kept.value(k - 2))
                    sp.sem_inc(passed_sp, 1)
                sp.dma_start(fx[:, par].rearrange("p j c -> p (j c)"), rows_dram[bass.ds(row, TILE)].rearrange("(p j) c -> p (j c)", p=P)).then_inc(fx_loaded[par].sem, 16)

            def load_weights(k, par):
                expert = sp.value_load(tile_expert_u[0:1, bass.ds(k, 1)], min_val=0, max_val=E - 1)
                if begun(k - 2):
                    sp.wait_ge(gelu_done.sem, gelu_done.value(k - 2))
                    sp.sem_inc(passed_sp, 1)
                sp.dma_start(w1_sb[:, par], w1[bass.ds(expert, 1)].rearrange("o (c p) i -> p (o c) i", p=P)).then_inc(w1_loaded[par].sem, 16)
                sp.dma_start(b1_sb[:, par], b1T[bass.ds(expert, 1)].rearrange("o p m -> p (o m)")).then_inc(w1_loaded[par].sem, 16)

            def load_tile(k, par):
                if tile_runs(k, -1):
                    load_rows(k + 1, 1 - par)
                    load_weights(k + 1, 1 - par)

            load_weights(0, 0)
            sp.wait_ge(padded, 16 * (E + 1))
            load_rows(0, 0)
            tile_steps(sp, load_tile)

        @block.tensor
        def _(pe):
            def latest(*readers):
                for sig, b, k in readers:
                    if not isinstance(b, int) or 0 <= b < B:
                        return sig.sem, sig.value(b, k)
                return consts_ready, VECTOR_CONSTS

            def transpose(dst, src, identity):
                return pe.transpose(dst, src, identity)

            def project(bank, lhs, rhs, n_out, width):
                for m in range(n_out):
                    for kc in range(KC):
                        last = pe.matmul(psum[:, bank, m * width:(m + 1) * width], lhs(kc, m), rhs(kc), start=(kc == 0), stop=(kc == KC - 1))
                return last

            def turn_z(i, lag, bank, src, ready, free, made):
                pe.wait_ge(*free)
                pe.wait_ge(ready.sem, ready.value(i - lag))
                for c in range(KC):
                    for t in range(NT):
                        last = transpose(psum[:, bank, c * T + t * P:c * T + (t + 1) * P], src[:, t, c * P:(c + 1) * P], ident)
                last.then_inc(made.sem, 1)

            def project_q(i, par):
                pe.wait_ge(zT_copied.sem, zT_copied.value(i))
                pe.wait_ge(*latest((yT_copied, i - 2, 1), (q_rest_made, i - 1, 1)))
                project(4, lambda kc, m: wqkv_sb[:, kc, m * P:(m + 1) * P], lambda kc: zT[:, kc, :], KC, T).then_inc(q_made.sem, 1)

            def project_k(i, par):
                pe.wait_ge(*latest((yT_copied, i - 2, 2), (k_rest_made, i - 1, 1)))
                project(5, lambda kc, m: wqkv_sb[:, kc, C + m * P:C + (m + 1) * P], lambda kc: zT[:, kc, :], KC, T).then_inc(k_made.sem, 1)

            def project_v(i, par):
                pe.wait_ge(*latest((y_scaled, i - 2, 1), (v_copied, i - 1, 1)))
                project(6, lambda kc, m: zT[:, kc, m * P:(m + 1) * P], lambda kc: wqkv_sb[:, kc, 2 * C:3 * C], NT, C).then_inc(v_made.sem, 1)

            def self_for_max(i, par, n):
                b, q = i - 1, 1 - par
                bank = S_BANKS[n % 2]
                if n == 0:
                    pe.wait_ge(q_packed[q].sem, q_packed[q].value(b // 2))
                    pe.wait_ge(k_packed[q].sem, k_packed[q].value(b // 2))
                    pe.wait_ge(*latest((cmxT_copied, i - 3, 1), (max_done, i - 2, 11)))
                elif n == 1:
                    pe.wait_ge(*latest((cmax_done, i - 3, 8), (ckv_copied, i - 2, 2)))
                else:
                    pe.wait_ge(max_done.sem, max_done.value(b, n - 1))
                if n < 4:
                    for j in range(4):
                        h = 4 * n + j
                        pe.matmul(psum[:, bank, j * P:(j + 1) * P], QP[0:KR, q, h, 0:P], KP[0:KR, q, h, 0:P], start=(j == 0), stop=False, skip_group_check=True)
                    diagonal = psum[:, bank, :]
                    masks = 4
                else:
                    for j in range(2):
                        h = 2 * (n - 4) + j
                        pe.matmul(psum[:, bank, j * T:(j + 1) * T], QP[0:KR, q, h, P:T], KP[0:KR, q, h, :], start=(j == 0), stop=False, skip_group_check=True)
                    diagonal = psum[:, bank, :].rearrange("p (j k) -> p j k", j=2)[:, :, P:T]
                    masks = 2
                pe.matmul(diagonal, ident_bf[:], mask_s[:].unsqueeze(1).broadcast_to([P, masks, P]), start=False, stop=True, skip_group_check=True).then_inc(s_made.sem, 1)

            def turn_max(i, lag, split, made, mx, bank):
                pe.wait_ge(split.sem, split.value(i - lag))
                for t in range(NT):
                    last = transpose(psum[0:2 * H, bank, 0:T // 2].bitcast(BF16)[:, t * P:(t + 1) * P], mx[:, t].rearrange("p y h -> p (y h)"), ident_bf[:])
                last.then_inc(made.sem, 1)

            def self_scores(i, par, n):
                b, q = i - 1, 1 - par
                KS = KR + 2
                g, r = divmod(n, 3)
                bank = ST_BANKS[n % 2]
                if n == 0:
                    pe.wait_ge(mx_packed[q].sem, mx_packed[q].value(b // 2))
                elif n == 1:
                    pe.wait_ge(*latest((cyC_copied, i - 3, 1), (exp_done, i - 2, 12)))
                else:
                    pe.wait_ge(exp_done.sem, exp_done.value(b, n - 1))
                if r < 2:
                    for j in range(2):
                        h = 4 * g + 2 * r + j
                        pe.matmul(psum[:, bank, j * T:(j + 1) * T], KP[0:KS, q, h, 0:P], QP[0:KS, q, h, :], start=(j == 0), stop=False, skip_group_check=True)
                    diagonal = psum[:, bank, :].rearrange("p (j k) -> p j k", j=2)[:, :, 0:P]
                    masks = 2
                else:
                    for j in range(4):
                        h = 4 * g + j
                        pe.matmul(psum[:, bank, j * P:(j + 1) * P], KP[0:KS, q, h, P:T], QP[0:KS, q, h, P:T], start=(j == 0), stop=False, skip_group_check=True)
                    diagonal = psum[:, bank, :]
                    masks = 4
                pe.matmul(diagonal, ident_bf[:], mask_t[:].unsqueeze(1).broadcast_to([P, masks, P]), start=False, stop=True, skip_group_check=True).then_inc(st_made.sem, 1)

            def self_values(i, par, g):
                b, q = i - 1, 1 - par
                bank, col = Y_BANKS[g // 2], (g % 2) * T
                if g == 0:
                    pe.wait_ge(v_copied.sem, v_copied.value(b))
                    pe.wait_ge(*latest((match_step, i - 2, 2 * NT), (q_rest_made, i, 1)))
                elif g == 2:
                    pe.wait_ge(*latest((kmask_made, i - 2, 1), (k_rest_made, i, 1)))
                pe.wait_ge(exp_done.sem, exp_done.value(b, 3 * g + 3))
                for j in range(4):
                    pe.matmul(psum[32 * j:32 * j + 32, bank, col:col + T], V[:, q, 0, 4 * g + j, :], PA[:, 4 * g + j, :], start=True, stop=False, skip_group_check=True)
                for j in range(4):
                    last = pe.matmul(psum[32 * j:32 * j + 32, bank, col + P:col + T], V[:, q, 1, 4 * g + j, :], PB[:, 4 * g + j, :], start=False, stop=True, skip_group_check=True)
                if g % 2 == 1:
                    last.then_inc(pv_made.sem, 1)

            def turn_y(i, lag, copied, free, made, src, banks):
                pe.wait_ge(copied.sem, copied.value(i - lag))
                for t in range(NT):
                    pe.wait_ge(*free[t])
                    for g in range(H // 4):
                        last = transpose(psum[:, banks[t], g * P:(g + 1) * P], src[:, g, t * P:(t + 1) * P], ident)
                    last.then_inc(made.sem, 1)

            def project_ctx(i, par):
                b, q = i - 1, 1 - par
                pe.wait_ge(ctx_loaded[q].sem, ctx_loaded[q].value(b // 2))
                pe.wait_ge(*latest((cy_scaled, i - 3, 2), (max_done, i - 1, 12)))
                for kc in range(KC):
                    pe.matmul(psum[0:KR, 1, 0:M], wmk_sb[:, kc, :], ctx_sb[:, q, kc, :], start=(kc == 0), stop=(kc == KC - 1))
                for kc in range(KC):
                    last = pe.matmul(psum[0:M, 1, P:P + D], ctx_sb[:, q, kc, :], wmv_sb[:, kc, :], start=(kc == 0), stop=(kc == KC - 1))
                last.then_inc(ckv_made.sem, 1)

            def project_cq(i, par):
                pe.wait_ge(czT_copied.sem, czT_copied.value(i - 2))
                pe.wait_ge(*latest((v_copied, i, 1), (y_scaled, i - 2, 1)))
                project(6, lambda kc, m: wq_sb[:, kc, m * P:(m + 1) * P], lambda kc: czT[:, kc, :], KC, T).then_inc(cq_made.sem, 1)

            def match(i, par):
                pe.wait_ge(*latest((cyT_copied, i - 3, 1), (q_rest_made, i, 1)))
                pe.wait_ge(cq_copied.sem, cq_copied.value(i - 2))
                project(4, lambda kc, m: cqT[:, kc * T + m * P:kc * T + (m + 1) * P], lambda kc: ctx_sb[:, par, kc, :], NT, M).then_inc(match_made.sem, 1)

            def counts(i, par):
                b = i - 2
                pe.wait_ge(*latest((cyT_copied, i - 3, 2), (k_rest_made, i, 1)))
                pe.wait_ge(onehot_made.sem, onehot_made.value(b))
                for t in range(NT):
                    pe.matmul(psum[0:M, 5, 0:1], onehot[:, t, :], ones_bf[:, 0:1], start=(t == 0), stop=(t == NT - 1))
                for t in range(NT):
                    last = pe.matmul(psum[:, 5, P:P + M], ones_bf[:], onehot[:, t, :], start=(t == 0), stop=(t == NT - 1))
                last.then_inc(count_made.sem, 1)

            def cross_for_max(i, par, n):
                b = i - 2
                KS = KR + 1
                t, g = divmod(n, 4)
                bank = S_BANKS[n % 2]
                if n == 0:
                    pe.wait_ge(cq_packed[par].sem, cq_packed[par].value(b // 2))
                    pe.wait_ge(kmask_made.sem, kmask_made.value(b))
                    pe.wait_ge(kc_step.sem, kc_step.value(b))
                if n == 0:
                    pe.wait_ge(*latest((cy_scaled, i - 3, 1), (max_done, i - 1, 11)))
                elif n == 1:
                    pe.wait_ge(*latest((ckv_copied, i - 1, 2), (cy_scaled, i - 3, 2)))
                else:
                    pe.wait_ge(cmax_done.sem, cmax_done.value(b, n - 1))
                for j in range(4):
                    last = pe.matmul(psum[:, bank, j * M:(j + 1) * M], QC[0:KS, par, 4 * g + j, t * P:(t + 1) * P], KCx[0:KS, par, 0:M], start=True, stop=True)
                last.then_inc(cs_made.sem, 1)

            def cross_scores(i, par, n):
                b, q = i - 3, 1 - par
                KS = KR + 3
                bank = ST_BANKS[n % 2]
                if n == 0:
                    pe.wait_ge(cmx_packed[q].sem, cmx_packed[q].value(b // 2))
                    pe.wait_ge(vc_made.sem, vc_made.value(b))
                    pe.wait_ge(*latest((zT_copied, i, 1), (exp_done, i - 2, 11), (cexp_done, i - 4, 7)))
                elif n == 1:
                    pe.wait_ge(*latest((rzT_copied, i - 4, 1), (exp_done, i - 2, 12)))
                else:
                    pe.wait_ge(cexp_done.sem, cexp_done.value(b, n - 1))
                pe.matmul(psum[0:M, bank, :], KCx[0:KS, q, 0:M], QC[0:KS, q, 2 * n:2 * n + 2, :], start=True, stop=True).then_inc(cst_made.sem, 1)

            def cross_values(i, par, g):
                b, q = i - 3, 1 - par
                bank, col = Y_BANKS[g // 2], (g % 2) * T
                if g == 0:
                    pe.wait_ge(*latest((q_rest_made, i, 1), (yT_copied, i - 2, 1), (match_step, i - 3, 2 * NT)))
                elif g == 2:
                    pe.wait_ge(*latest((k_rest_made, i, 1), (yT_copied, i - 2, 2), (kmask_made, i - 3, 1)))
                pe.wait_ge(cexp_done.sem, cexp_done.value(b, 2 * g + 2))
                for j in range(4):
                    last = pe.matmul(psum[32 * j:32 * j + 32, bank, col:col + T], VC[0:M, q, :], PC[0:M, 4 * g + j, :], start=True, stop=True)
                if g % 2 == 1:
                    last.then_inc(cpv_made.sem, 1)

            def project_out(i, par):
                b = i - 3
                pe.wait_ge(*latest((cq_copied, i - 2, 1), (x2_made, i - 4, 1)))
                pe.wait_ge(cyC_copied.sem, cyC_copied.value(b))
                project(6, lambda kc, m: cyC[:, kc, m * P:(m + 1) * P], lambda kc: wc_sb[:, kc, :], NT, C).then_inc(o_made.sem, 1)

            def logits(i, par):
                b = i - 4
                pe.wait_ge(*latest((czT_copied, i - 2, 1), (place_step, i - 5, 5)))
                pe.wait_ge(rzT_copied.sem, rzT_copied.value(b))
                for t in range(NT):
                    for kc in range(KC):
                        last = pe.matmul(psum[:, 7, t * E:(t + 1) * E], rzT[:, kc, t * P:(t + 1) * P], wr_sb[:, kc, :], start=(kc == 0), stop=(kc == KC - 1))
                last.then_inc(logits_made.sem, 1)

            def rank(i, par):
                b = i - 4
                pe.wait_ge(route_step.sem, route_step.value(b))
                pe.matmul(psum[:, 7, 0:E], before_bf[:], chosen_bf[:, 0, :], start=True, stop=True)
                pe.matmul(psum[:, 7, E:2 * E], before_bf[:], chosen_bf[:, 1, :], start=True, stop=False)
                pe.matmul(psum[:, 7, E:2 * E], ones_bf[:], chosen_bf[:, 0, :], start=False, stop=True)
                pe.matmul(psum[:, 7, 2 * E:3 * E], ones_bf[:], chosen_bf[:, 0, :], start=True, stop=False)
                pe.matmul(psum[:, 7, 2 * E:3 * E], ones_bf[:], chosen_bf[:, 1, :], start=False, stop=True).then_inc(rank_made.sem, 1)

            def body(i, par):
                if isinstance(i, int) and i == 1:
                    pe.wait_ge(weights_in, 16 * N_WEIGHT_LOADS)
                    pe.wait_ge(gpsimd_consts, GPSIMD_CONSTS)
                if runs(i, 0):
                    turn_z(i, 0, 2, z, ln1_step, latest((exp_done, i - 2, 11), (zT_copied, i - 1, 1)), xT_made)
                if runs(i, 4):
                    turn_z(i, 4, 3, rz, ln3_step, latest((exp_done, i - 2, 12), (cyC_copied, i - 4, 1)), rzT_made)
                if runs(i, 0):
                    project_q(i, par)
                    project_k(i, par)
                    project_v(i, par)
                for g in range(4):
                    if g == 1 and runs(i, 2):
                        turn_z(i, 2, 7, cz, ln2_step, latest((y_scaled, i - 2, 2)), czT_made)
                    if g == 3 and runs(i, 2):
                        project_cq(i, par)
                    for r in range(3):
                        if runs(i, 1):
                            self_for_max(i, par, 3 * g + r)
                        if runs(i, 3) and r < 2:
                            cross_scores(i, par, 2 * g + r)
                    if runs(i, 3) and g > 0:
                        cross_values(i, par, g - 1)
                if runs(i, 3):
                    cross_values(i, par, 3)
                if runs(i, 2):
                    match(i, par)
                if runs(i, 3):
                    turn_y(i, 3, cyT_copied, (latest((max_done, i - 1, 11), (cmxT_copied, i - 3, 1)), latest((max_done, i - 1, 12), (cmax_done, i - 3, 8))), cyt_made, cyT, (0, 1))
                if runs(i, 1):
                    pe.wait_ge(*latest((cexp_done, i - 3, 7), (zT_copied, i, 1)))
                    turn_max(i, 1, mx_split, mxT_made, mx2, 2)
                if runs(i, 4):
                    logits(i, par)
                if runs(i, 3):
                    turn_z(i, 3, 3, cy, cy_scaled, latest((cexp_done, i - 3, 8)), cyC_made)
                if runs(i, 1):
                    project_ctx(i, par)
                if runs(i, 3):
                    project_out(i, par)
                if runs(i, 2):
                    counts(i, par)
                for g in range(4):
                    for r in range(3):
                        if runs(i, 1):
                            self_scores(i, par, 3 * g + r)
                        if runs(i, 2) and g > 0 and 3 * (g - 1) + r < 8:
                            cross_for_max(i, par, 3 * (g - 1) + r)
                    if runs(i, 1) and g > 0:
                        self_values(i, par, g - 1)
                    if runs(i, 4) and g == 0:
                        rank(i, par)
                if runs(i, 1):
                    self_values(i, par, 3)
                if runs(i, 2):
                    turn_max(i, 2, cmx_split, cmxT_made, cmx2, 0)
                if runs(i, 1):
                    turn_y(i, 1, yT_copied, (latest((x2_made, i - 3, 1), (cq_copied, i - 2, 1), (v_copied, i, 1)), latest((place_step, i - 4, 5), (czT_copied, i - 2, 1))), yt_made, yT, (6, 7))

            pe.wait_ge(consts_ready, VECTOR_CONSTS)
            pe.wait_ge(first_weights_in, 16 * N_FIRST_LOADS)
            steps(pe, body)

            pe.wait_ge(rank_made.sem, rank_made.value(B - 1))
            pe.wait_ge(rzT_copied.sem, rzT_copied.value(B - 1))
            pe.wait_ge(place_step.sem, place_step.value(B - 1))
            pe.wait_ge(kc_step.sem, kc_step.value(B - 1))
            pe.wait_ge(ln3_rstd.sem, ln3_rstd.value(B - 1))
            for par in range(2):
                pe.wait_ge(x_loaded[par].sem, x_loaded[par].value(B // 2))
                pe.wait_ge(rows_sent[par].sem, rows_sent[par].value(B // 2 - 1))

            pe.wait_ge(wo_split, 4)

            def turn_tile(k, par):
                pe.wait_ge(fln_step.sem, fln_step.value(k))
                for kc in range(KC):
                    if begun(k - 1):
                        pe.wait_ge(fzT_copied.sem, fzT_copied.value(k - 1, kc + 1))
                    for j in range(TS):
                        last = transpose(psum[:, 6 + kc, j * P:(j + 1) * P], fz[:, j, kc * P:(kc + 1) * P], ident)
                    last.then_inc(fzT_made.sem, 1)

            def widen(k, par):
                b, q = k - 1, 1 - par
                pe.wait_ge(w1_low_made.sem, w1_low_made.value(b))
                pe.wait_ge(z_low_made.sem, z_low_made.value(b))
                for m in range(MI):
                    bank = m % 4
                    if m >= 4:
                        pe.wait_ge(gelu_done.sem, gelu_done.value(b, m - 3))
                    elif begun(b - 1):
                        pe.wait_ge(gelu_done.sem, gelu_done.value(b - 1, m + 5))
                    cols = slice(m * P, (m + 1) * P)
                    products = [pair for kc in range(KC) for pair in (
                        (w1_low[:, q, kc, cols], fzT_high[:, kc, :]),
                        (w1_high[:, q, kc, cols], fzT_low[:, kc, :]),
                        (w1_high[:, q, kc, cols], fzT_high[:, kc, :]))]
                    for n, (lhs, rhs) in enumerate(products):
                        last = pe.matmul(psum[:, bank, :], lhs, rhs, start=(n == 0), stop=(n == len(products) - 1))
                    last.then_inc(h_made.sem, 1)

            def narrow(k, par):
                b = k - 1
                for half in range(2):
                    if begun(b - 1):
                        pe.wait_ge(ysum_made.sem, ysum_made.value(b - 1, half + 1))
                    for j in range(2):
                        for m in range(MI):
                            if half == 0 and j == 0 and m in H_LOW_POOL:
                                pe.wait_ge(h_low_pool.sem, h_low_pool.value(b, H_LOW_POOL.index(m) + 1))
                            elif half == 0 and j == 0:
                                pe.wait_ge(h_low_dve.sem, h_low_dve.value(b, H_LOW_DVE.index(m) + 1))
                            rows = slice((2 * half + j) * P, (2 * half + j + 1) * P)
                            for n, (lhs, rhs) in enumerate(((hT_low[:, m, rows], wo_high[:, m, :]), (hT_high[:, m, rows], wo_low[:, m, :]), (hT_high[:, m, rows], wo_high[:, m, :]))):
                                last = pe.matmul(psum[:, 4 + half, j * C:(j + 1) * C], lhs, rhs, start=(m == 0 and n == 0), stop=(m == MI - 1 and n == 2))
                    last.then_inc(ffn_made.sem, 1)

            def tile_body(k, par):
                if tile_runs(k, 1):
                    widen(k, par)
                if tile_runs(k, 0):
                    turn_tile(k, par)
                if tile_runs(k, 1):
                    narrow(k, par)

            tile_steps(pe, tile_body)

        @block.scalar
        def _(act):
            def copy(dst, src):
                return act.activation(dst, src, ACT.Copy)

            def copy_z(i, lag, made, free, dst, bank, copied):
                act.wait_ge(made.sem, made.value(i - lag))
                if begun(i - lag - 1):
                    act.wait_ge(free.sem, free.value(i - lag - 1))
                copy(dst[:].rearrange("p c n -> p (c n)"), psum[:, bank, :]).then_inc(copied.sem, 1)

            def stage_A(i, par):
                for made, stored, parts, high, bank, bias in ((q_made, q_stored, q_parts, q_high, 4, 0), (k_made, k_stored, k_parts, k_high, 5, KC)):
                    act.wait_ge(made.sem, made.value(i))
                    if begun(i - 1):
                        act.wait_ge(stored[1 - par].sem, stored[1 - par].value((i - 1) // 2))
                    for c in range(KC):
                        last = act.activation(parts[:, 0, c * T:(c + 1) * T], psum[:, bank, c * T:(c + 1) * T], ACT.Identity, bias=bqk_sb[:, bias + c:bias + c + 1])
                    last.then_inc(high.sem, 1)
                for made, parts, rest, mid in ((q_rest_made, q_parts, q_rest, q_mid), (k_rest_made, k_parts, k_rest, k_mid)):
                    act.wait_ge(made.sem, made.value(i))
                    copy(parts[:, 1, :], rest[:]).then_inc(mid.sem, 1)

            def copy_max(b, par, made, filled, packed, mx_t, bank, copied, dst, row):
                act.wait_ge(made.sem, made.value(b))
                if begun(b - 1):
                    act.wait_ge(packed[1 - par].sem, packed[1 - par].value((b - 1) // 2))
                copy(mx_t[:], psum[0:2 * H, bank, 0:T // 2].bitcast(BF16)).then_inc(copied.sem, 1)
                if dst is None:
                    return
                act.wait_ge(copied.sem, copied.value(b))
                act.sem_inc(passed_act, 1)
                act.wait_ge(filled[par].sem, filled[par].value(b // 2))
                act.sem_inc(passed_act, 1)
                for part in range(2):
                    act.dma_start(dst[row + part:row + part + 1, par], mx_t[H * part:H * part + H, :]).then_inc(packed[par].sem, 16)

            def self_exp(i, par):
                b = i - 1
                if begun(b - 1):
                    act.wait_ge(pv_made.sem, pv_made.value(b - 1))
                for n in range(12):
                    g, r = divmod(n, 3)
                    act.wait_ge(st_made.sem, st_made.value(b, n + 1))
                    if r < 2:
                        h = 4 * g + 2 * r
                        dst = PA[:, h:h + 2, :].rearrange("p h n -> p (h n)")
                    else:
                        dst = PB[:, 4 * g:4 * g + 4, :].rearrange("p h n -> p (h n)")
                    act.activation(dst, psum[:, ST_BANKS[n % 2], :], ACT.Exp, scale=D ** -0.5).then_inc(exp_done.sem, 1)
                if begun(b - 1):
                    act.wait_ge(yt_made.sem, yt_made.value(b - 1))
                for n in range(2):
                    act.wait_ge(pv_made.sem, pv_made.value(b, n + 1))
                    copy(yT[:, 2 * n:2 * n + 2, :].rearrange("p g n -> p (g n)"), psum[:, Y_BANKS[n], :]).then_inc(yT_copied.sem, 1)

            def cross_exp(i, par, n):
                b = i - 3
                if n == 0 and begun(b - 1):
                    act.wait_ge(cpv_made.sem, cpv_made.value(b - 1))
                act.wait_ge(cst_made.sem, cst_made.value(b, n + 1))
                act.activation(PC[0:M, 2 * n:2 * n + 2, :].rearrange("p h n -> p (h n)"), psum[0:M, ST_BANKS[n % 2], :], ACT.Exp, scale=D ** -0.5).then_inc(cexp_done.sem, 1)

            def copy_cy(i, par):
                b = i - 3
                if begun(b - 1):
                    act.wait_ge(cyt_made.sem, cyt_made.value(b - 1))
                for n in range(2):
                    act.wait_ge(cpv_made.sem, cpv_made.value(b, n + 1))
                    copy(cyT[:, 2 * n:2 * n + 2, :].rearrange("p g n -> p (g n)"), psum[:, Y_BANKS[n], :]).then_inc(cyT_copied.sem, 1)

            def copy_ctx(i, par):
                b = i - 1
                act.wait_ge(ckv_made.sem, ckv_made.value(b))
                if begun(b - 1):
                    act.wait_ge(kc_step.sem, kc_step.value(b - 1))
                if begun(b - 2):
                    act.wait_ge(vc_made.sem, vc_made.value(b - 2))
                copy(kc32[0:KR, :], psum[0:KR, 1, 0:M]).then_inc(ckv_copied.sem, 1)
                copy(cv[0:M, 1 - par, :], psum[0:M, 1, P:P + D]).then_inc(ckv_copied.sem, 1)

            def copy_cq(i, par):
                b = i - 2
                act.wait_ge(cq_made.sem, cq_made.value(b))
                if begun(b - 1):
                    act.wait_ge(match_made.sem, match_made.value(b - 1))
                    act.wait_ge(cq_rest_made.sem, cq_rest_made.value(b - 1))
                copy(cqT[:], psum[:, 6, :]).then_inc(cq_copied.sem, 1)
                act.wait_ge(cq_copied.sem, cq_copied.value(b))
                if begun(b - 1):
                    act.wait_ge(cq_stored[1 - par].sem, cq_stored[1 - par].value((b - 1) // 2))
                copy(cq_parts[:, 0, :], cqT[:]).then_inc(cq_high.sem, 1)

            def body(i, par):
                if runs(i, 0):
                    copy_z(i, 0, xT_made, v_made, zT, 2, zT_copied)
                if runs(i, 4):
                    copy_z(i, 4, rzT_made, logits_made, rzT, 3, rzT_copied)
                if runs(i, 0):
                    stage_A(i, par)
                for n in range(8):
                    if n == 2 and runs(i, 2):
                        copy_z(i, 2, czT_made, cq_made, czT, 7, czT_copied)
                    if n == 6 and runs(i, 2):
                        copy_cq(i, par)
                    if runs(i, 3):
                        cross_exp(i, par, n)
                if runs(i, 2):
                    act.wait_ge(cq_rest_made.sem, cq_rest_made.value(i - 2))
                    copy(cq_parts[:, 1, :], cq_rest[:]).then_inc(cq_mid.sem, 1)
                if runs(i, 3):
                    copy_cy(i, par)
                if runs(i, 1):
                    copy_max(i - 1, 1 - par, mxT_made, q_packed, mx_packed, mxT, 2, mxT_copied, QP, KR)
                if runs(i, 3):
                    copy_z(i, 3, cyC_made, o_made, cyC, 3, cyC_copied)
                if runs(i, 1):
                    copy_ctx(i, par)
                if runs(i, 1):
                    self_exp(i, par)
                if runs(i, 2):
                    copy_max(i - 2, par, cmxT_made, cq_packed, cmx_packed, cmxT, 0, cmxT_copied, None, None)
            act.wait_ge(first_weights_in, 16 * N_FIRST_LOADS)
            steps(act, body)

            act.wait_ge(rank_made.sem, rank_made.value(B - 1))
            act.wait_ge(rzT_copied.sem, rzT_copied.value(B - 1))
            act.wait_ge(place_step.sem, place_step.value(B - 1))
            act.wait_ge(kc_step.sem, kc_step.value(B - 1))
            act.wait_ge(ln3_rstd.sem, ln3_rstd.value(B - 1))
            for par in range(2):
                act.wait_ge(x_loaded[par].sem, x_loaded[par].value(B // 2))
                act.wait_ge(rows_sent[par].sem, rows_sent[par].value(B // 2 - 1))

            def tile_body(k, par):
                if tile_runs(k, 1):
                    b, q = k - 1, 1 - par
                    act.wait_ge(w1_loaded[q].sem, w1_loaded[q].value(b // 2))
                    if begun(b - 1):
                        act.wait_ge(ffn_made.sem, ffn_made.value(b - 1))
                    for m in range(MI):
                        act.wait_ge(h_made.sem, h_made.value(b, m + 1))
                        act.activation(hT[:, m, :], psum[:, m % 4, :], ACT.Gelu, bias=b1_sb[:, q, m:m + 1]).then_inc(gelu_done.sem, 1)
                if tile_runs(k, 0):
                    if begun(k - 1):
                        act.wait_ge(h_made.sem, h_made.value(k - 1))
                    for kc in range(KC):
                        act.wait_ge(fzT_made.sem, fzT_made.value(k, kc + 1))
                        copy(fzT[:, kc, :], psum[:, 6 + kc, :]).then_inc(fzT_copied.sem, 1)

            tile_steps(act, tile_body)

        @block.vector
        def _(dve):
            made = [0]

            def constant(ins):
                ins.then_inc(consts_ready, 1)
                made[0] += 1

            dve.wait_ge(consts_in, 16)
            constant(dve.tensor_copy(ident_bf[:], consts_sb[:, 0:P]))
            constant(dve.tensor_copy(mask_s[:], consts_sb[:, P:2 * P]))
            constant(dve.tensor_copy(mask_t[:], consts_sb[:, 2 * P:3 * P]))
            constant(dve.memset(ones_bf[:], 1.0))
            constant(dve.tensor_copy(before_bf[:], consts_sb[:, BEFORE:BEFORE + P]))
            constant(dve.tensor_copy(next_row[:], consts_sb[:, NEXT_ROW:NEXT_ROW + E]))
            for par in range(2):
                constant(dve.tensor_copy(x2[:, par, :, C], consts_sb[:, NUMBERS + par * NT:NUMBERS + (par + 1) * NT]))
            constant(dve.memset(minus_half[:], -0.5))
            assert made[0] == VECTOR_CONSTS

            def ln_statistics(b, src, st, mean_var, step, NT=NT):
                for t in range(NT):
                    dve.bn_stats(st[:, t, :], src[:, t, :]).then_inc(step.sem, 1)
                for t in range(NT):
                    dve.wait_ge(step.sem, step.value(b, t + 1))
                    dve.sem_inc(passed_dve, 1)
                    dve.bn_aggr(mean_var[:, t, :], st[:, t, :]).then_inc(step.sem, 1)

            def ln_normalize(b, src, dst, mean_var, step, rs, rstd_made, NT=NT):
                dve.wait_ge(rstd_made.sem, rstd_made.value(b))
                for t in range(NT):
                    dve.tensor_scalar(dst[:, t, :], src[:, t, :], mean_var[:, t, 0:1], rs[:, t:t + 1], ALU.subtract, ALU.mult).then_inc(step.sem, 1)

            def split_max(b, done, top, mx, turned, split):
                dve.wait_ge(done.sem, done.value(b))
                if begun(b - 1):
                    dve.wait_ge(turned.sem, turned.value(b - 1))
                dve.tensor_scalar(mx[:, :, 0, :], top[:], -1.0, None, ALU.mult).then_inc(split.sem, 1)
                dve.wait_ge(split.sem, split.value(b, 1))
                dve.scalar_tensor_tensor(mx[:, :, 1, :], top[:], -1.0, mx[:, :, 0, :], ALU.mult, ALU.subtract).then_inc(split.sem, 1)

            def self_max(i, par):
                b = i - 1
                for n in range(12):
                    if n == 11 and runs(i, 2):
                        split_cq(i, par)
                    dve.wait_ge(s_made.sem, s_made.value(b, n + 1))
                    bank = psum[:, S_BANKS[n % 2], :]
                    if n < 4:
                        dve.tensor_reduce(negmax[:, 0, 4 * n:4 * n + 4], bank.rearrange("p (h k) -> p h k", h=4), AX_X, ALU.max).then_inc(max_done.sem, 1)
                    else:
                        h = 2 * (n - 4)
                        dve.tensor_reduce(negmax[:, 1, h:h + 2], bank.rearrange("p (h k) -> p h k", h=2), AX_X, ALU.max).then_inc(max_done.sem, 1)
                split_max(b, max_done, negmax, mx2, mxT_made, mx_split)

            def cross_max(i, par, n):
                b = i - 2
                t, g = divmod(n, 4)
                dve.wait_ge(cs_made.sem, cs_made.value(b, n + 1))
                dve.tensor_reduce(cnegmax[:, t, 4 * g:4 * g + 4], psum[:, S_BANKS[n % 2], 0:4 * M].rearrange("p (h k) -> p h k", h=4), AX_X, ALU.max).then_inc(cmax_done.sem, 1)

            def ln1_statistics(b, par):
                dve.wait_ge(x_loaded[par].sem, x_loaded[par].value(b // 2))
                ln_statistics(b, x_in[:, par], stats, mv, ln1_step)

            def ln1_normalize(b, par):
                if begun(b - 1):
                    dve.wait_ge(xT_made.sem, xT_made.value(b - 1))
                ln_normalize(b, x_in[:, par], z, mv, ln1_step, rstd, ln1_rstd)

            def stage_A2(i, par):
                for high, low, mid, parts, rest, bank, bias, rest_made in ((q_high, q_low, q_mid, q_parts, q_rest, 4, 0, q_rest_made), (k_high, k_low, k_mid, k_parts, k_rest, 5, KC, k_rest_made)):
                    dve.wait_ge(high.sem, high.value(i))
                    if begun(i - 1):
                        dve.wait_ge(low.sem, low.value(i - 1))
                        dve.wait_ge(mid.sem, mid.value(i - 1))
                    for c in range(KC):
                        cols = slice(c * T, (c + 1) * T)
                        last = dve.scalar_tensor_tensor(rest[:, cols], psum[:, bank, cols], bqk_sb[:, bias + c:bias + c + 1], parts[:, 0, cols], ALU.add, ALU.subtract)
                    last.then_inc(rest_made.sem, 1)

            def add_v_bias(i, par):
                dve.wait_ge(v_made.sem, v_made.value(i))
                if begun(i - 2):
                    dve.wait_ge(pv_made.sem, pv_made.value(i - 2))
                for t in range(NT):
                    last = dve.tensor_tensor(V[:, par, t, :, 0:D].rearrange("p (h c) d -> p c h d", c=KC), psum[:, 6, t * C:(t + 1) * C].rearrange("p (c h d) -> p c h d", c=KC, h=HP),
                                             bv_sb[:].rearrange("p (c h d) -> p c h d", c=KC, h=HP), ALU.add)
                last.then_inc(v_copied.sem, 1)

            def scale_rows(b, made, free, rs, summed, dst, scaled, banks):
                for t in range(NT):
                    heads = psum[:, banks[t], :].rearrange("p (h e) -> p h e", e=2 * D)
                    dve.wait_ge(made.sem, made.value(b, t + 1))
                    dve.reciprocal(rs[:, t, :], heads[:, :, D]).then_inc(summed.sem, 1)
                    dve.wait_ge(summed.sem, summed.value(b, t + 1))
                    if free is not None:
                        if begun(b - 1):
                            dve.wait_ge(free.sem, free.value(b - 1))
                    dve.tensor_tensor(dst[:, t, :].rearrange("p (c h d) -> p c h d", c=KC, h=HP),
                                      heads[:, :, 0:D].rearrange("p (h c) d -> p c h d", c=KC),
                                      rs[:, t, :].rearrange("p (h c) -> p c h", c=KC).unsqueeze(3).broadcast_to([P, KC, HP, D]), ALU.mult).then_inc(scaled.sem, 1)

            def residual_1(i, par):
                b, q = i - 1, 1 - par
                scale_rows(b, yt_made, None, rsum, rsum_made, y, y_scaled, (6, 7))
                dve.wait_ge(xres_loaded[q].sem, xres_loaded[q].value(b // 2))
                if begun(b - 2):
                    dve.wait_ge(x2_made.sem, x2_made.value(b - 2))
                for t in range(NT):
                    dve.wait_ge(y_scaled.sem, y_scaled.value(b, t + 1))
                    dve.tensor_tensor(x1[:, q, t, :], y[:, t, :], x_res[:, q, t, :], ALU.add).then_inc(x1_made.sem, 1)
                dve.wait_ge(x1_made.sem, x1_made.value(b))
                ln_statistics(b, x1[:, q], cstats, cmv, ln2_step)
                if begun(b - 1):
                    dve.wait_ge(czT_made.sem, czT_made.value(b - 1))
                ln_normalize(b, x1[:, q], cz, cmv, ln2_step, crstd, ln2_rstd)

            def split_cq(i, par):
                b = i - 2
                dve.wait_ge(cq_high.sem, cq_high.value(b))
                if begun(b - 1):
                    dve.wait_ge(cq_low.sem, cq_low.value(b - 1))
                    dve.wait_ge(cq_mid.sem, cq_mid.value(b - 1))
                dve.tensor_tensor(cq_rest[:], cqT[:], cq_parts[:, 0, :], ALU.subtract).then_inc(cq_rest_made.sem, 1)

            def choose(i, par):
                b = i - 2
                dve.wait_ge(match_made.sem, match_made.value(b))
                dve.sem_inc(passed_dve, 1)
                for t in range(NT):
                    dve.max(top8[:, t, :], psum[:, 4, t * M:(t + 1) * M]).then_inc(match_step.sem, 1)
                for t in range(NT):
                    dve.wait_ge(match_step.sem, match_step.value(b, t + 1))
                    dve.sem_inc(passed_dve, 1)
                    dve.max_index(top8i[:, t, :], top8[:, t, :], psum[:, 4, t * M:(t + 1) * M]).then_inc(match_step.sem, 1)
                dve.wait_ge(match_step.sem, match_step.value(b, 2 * NT))
                dve.tensor_copy(first[:], top8i[:, :, 0]).then_inc(match_step.sem, 1)
                dve.wait_ge(match_step.sem, match_step.value(b))
                if begun(b - 1):
                    dve.wait_ge(count_made.sem, count_made.value(b - 1))
                for t in range(NT):
                    dve.tensor_scalar(onehot[:, t, :], iota_m, first[:, t:t + 1], None, ALU.is_equal).then_inc(onehot_made.sem, 1)

            def weigh(i, par):
                b = i - 2
                dve.wait_ge(count_made.sem, count_made.value(b))
                dve.tensor_copy(cnt_sb[0:M, :], psum[0:M, 5, 0:1]).then_inc(count_copied.sem, 1)
                if begun(b - 2):
                    dve.wait_ge(cst_made.sem, cst_made.value(b - 2))
                dve.tensor_scalar(KCx[KR:KR + 1, par, 0:M], psum[KR:KR + 1, 5, P:P + M], 0.0, NEG, ALU.is_equal, ALU.mult).then_inc(kmask_made.sem, 1)
                dve.wait_ge(count_copied.sem, count_copied.value(b))
                dve.wait_ge(ckv_copied.sem, ckv_copied.value(b))
                if begun(b - 2):
                    dve.wait_ge(cpv_made.sem, cpv_made.value(b - 2))
                dve.tensor_scalar(VC[0:M, par, 0:D], cv[0:M, par, :], cnt_sb[0:M, 0:1], None, ALU.mult).then_inc(vc_made.sem, 1)
                dve.tensor_copy(VC[0:M, par, D:D + 1], cnt_sb[0:M, :]).then_inc(vc_made.sem, 1)

            def residual_2(i, par):
                b, q = i - 3, 1 - par
                dve.wait_ge(o_made.sem, o_made.value(b))
                if begun(b - 2):
                    dve.wait_ge(rows_sent[q].sem, rows_sent[q].value((b - 2) // 2))
                dve.tensor_tensor(x2[:, q, :, 0:C], psum[:, 6, :].rearrange("p (t c) -> p t c", t=NT), x1[:, q], ALU.add).then_inc(x2_made.sem, 1)
                dve.tensor_scalar(x2[:, q, :, C], x2[:, q, :, C], 2.0 * T, None, ALU.add).then_inc(number_made.sem, 1)
                dve.wait_ge(x2_made.sem, x2_made.value(b))
                ln_statistics(b, x2[:, q, :, 0:C], rstats, rmv, ln3_step)

            def ln3_normalize(i, par):
                b, q = i - 3, 1 - par
                if begun(b - 1):
                    dve.wait_ge(rzT_made.sem, rzT_made.value(b - 1))
                ln_normalize(b, x2[:, q, :, 0:C], rz, rmv, ln3_step, rrstd, ln3_rstd)

            def route(i, par):
                b = i - 4
                dve.wait_ge(logits_made.sem, logits_made.value(b))
                lg = psum[:, 7, 0:NT * E].rearrange("p (t e) -> p t e", t=NT)

                def spread(a):
                    return a[:].unsqueeze(2).broadcast_to([P, NT, E])
                dve.tensor_reduce(greatest[:], lg, AX_X, ALU.max).then_inc(route_step.sem, 1)
                dve.wait_ge(route_step.sem, route_step.value(b, 1))
                dve.tensor_tensor(equal[:], lg, spread(greatest), ALU.is_equal).then_inc(route_step.sem, 1)
                dve.wait_ge(route_step.sem, route_step.value(b, 2))
                dve.tensor_tensor(equal[:], equal[:], prefer.unsqueeze(1).broadcast_to([P, NT, E]), ALU.mult).then_inc(route_step.sem, 1)
                dve.wait_ge(route_step.sem, route_step.value(b, 3))
                dve.tensor_reduce(greatest[:], equal[:], AX_X, ALU.max).then_inc(route_step.sem, 1)
                dve.wait_ge(route_step.sem, route_step.value(b, 4))
                dve.tensor_tensor(chosen[:], equal[:], spread(greatest), ALU.is_equal).then_inc(route_step.sem, 1)
                if begun(b - 1):
                    dve.wait_ge(rank_made.sem, rank_made.value(b - 1))
                dve.wait_ge(route_step.sem, route_step.value(b, 5))
                dve.tensor_copy(chosen_bf[:], chosen[:]).then_inc(route_step.sem, 1)

            def find_rows(i, par):
                b = i - 4
                dve.wait_ge(rank_made.sem, rank_made.value(b))
                if begun(b - 1):
                    dve.wait_ge(place_step.sem, place_step.value(b - 1))
                dve.tensor_tensor(place[:], psum[:, 7, 0:NT * E].rearrange("p (t e) -> p t e", t=NT), next_row[:].unsqueeze(1).broadcast_to([P, NT, E]), ALU.add).then_inc(place_step.sem, 1)
                dve.wait_ge(place_step.sem, place_step.value(b, 1))
                dve.tensor_tensor(place[:], place[:], chosen[:], ALU.mult).then_inc(place_step.sem, 1)
                dve.wait_ge(place_step.sem, place_step.value(b, 2))
                dve.tensor_reduce(row_no[:], place[:], AX_X, ALU.add).then_inc(place_step.sem, 1)
                dve.wait_ge(place_step.sem, place_step.value(b, 3))
                if begun(b - 2):
                    dve.wait_ge(rows_sent[par].sem, rows_sent[par].value((b - 2) // 2))
                dve.tensor_copy(row_u[:, par, :], row_no[:]).then_inc(place_step.sem, 1)
                dve.tensor_tensor(next_row[:], psum[:, 7, NT * E:(NT + 1) * E], next_row[:], ALU.add).then_inc(place_step.sem, 1)

            def body(i, par):
                if runs(i, 0):
                    stage_A2(i, par)
                    add_v_bias(i, par)
                if runs(i, 1):
                    self_max(i, par)
                elif runs(i, 2):
                    split_cq(i, par)
                if runs(i, 3):
                    scale_rows(i - 3, cyt_made, cyC_made, crsum, crsum_made, cy, cy_scaled, (0, 1))
                if runs(i, 2):
                    choose(i, par)
                if runs(i, 4):
                    route(i, par)
                if runs(i, 2):
                    weigh(i, par)
                if runs(i, 3):
                    residual_2(i, par)
                for n in range(8):
                    if runs(i, 2):
                        cross_max(i, par, n)
                    if n == 1 and runs(i, 3):
                        ln3_normalize(i, par)
                    if n == 3 and runs(i, 4):
                        find_rows(i, par)
                    if n == 5 and runs(i, 0):
                        ln1_statistics(i + 1, 1 - par)
                if runs(i, 2):
                    split_max(i - 2, cmax_done, cnegmax, cmx2, cmxT_made, cmx_split)
                if runs(i, 0):
                    ln1_normalize(i + 1, 1 - par)
                if runs(i, 1):
                    residual_1(i, par)

            dve.wait_ge(consts_ready, VECTOR_CONSTS)
            ln1_statistics(0, 0)
            ln1_normalize(0, 0)
            dve.wait_ge(gpsimd_consts, 3)
            dve.wait_ge(first_weights_in, 16 * N_FIRST_LOADS)
            steps(dve, body)

            planned = [0]

            def plan(ins):
                ins.then_inc(plan_step, 1)
                planned[0] += 1
                dve.wait_ge(plan_step, planned[0])

            first_row = consts_sb[:, NEXT_ROW:NEXT_ROW + E]
            tile_nos = consts_sb[:, TILE_NOS:TILE_NOS + TILES]
            dve.wait_ge(place_step.sem, place_step.value(B - 1))
            plan(dve.tensor_tensor(count_f[:], next_row[:], first_row, ALU.subtract))
            plan(dve.tensor_scalar(count_i[:], count_f[:], float(TILE - 1), None, ALU.add))
            plan(dve.tensor_scalar(count_i[:], count_i[:], TILE.bit_length() - 1, None, ALU.logical_shift_right))
            plan(dve.tensor_copy(tiles_f[:], count_i[:]))
            plan(dve.tensor_scalar(jump[:], tiles_f[:], -float(TILE), float(ROOM), ALU.mult, ALU.add))
            for e in range(1, E):
                plan(dve.tensor_tensor(tiles_f[:, e:e + 1], tiles_f[:, e:e + 1], tiles_f[:, e - 1:e], ALU.add))
            plan(dve.tensor_scalar(tile_row[:], tile_nos, float(TILE), None, ALU.mult))
            for e in range(E):
                plan(dve.tensor_scalar(past[:, e, :], tile_nos, tiles_f[:, e:e + 1], None, ALU.is_ge))
                plan(dve.scalar_tensor_tensor(tile_row[:], past[:, e, :], jump[:, e:e + 1], tile_row[:], ALU.mult, ALU.add))
                if e:
                    plan(dve.tensor_tensor(tile_expert[:], tile_expert[:] if e > 1 else past[:, 0, :], past[:, e, :], ALU.add))
            plan(dve.tensor_scalar(tile_row_u[:, 0:TILES], tile_row[:], float(E * ROOM), None, ALU.min))
            plan(dve.tensor_scalar(tile_expert_u[:, 0:TILES], tile_expert[:], float(E - 1), None, ALU.min))
            plan(dve.tensor_copy(next_u[:], next_row[:]))
            assert planned[0] == PLAN_STEPS

            dve.wait_ge(rank_made.sem, rank_made.value(B - 1))
            dve.wait_ge(rzT_copied.sem, rzT_copied.value(B - 1))
            dve.wait_ge(place_step.sem, place_step.value(B - 1))
            dve.wait_ge(kc_step.sem, kc_step.value(B - 1))
            dve.wait_ge(ln3_rstd.sem, ln3_rstd.value(B - 1))
            for par in range(2):
                dve.wait_ge(x_loaded[par].sem, x_loaded[par].value(B // 2))
                dve.wait_ge(rows_sent[par].sem, rows_sent[par].value(B // 2 - 1))

            dve.wait_ge(weights_in, 16 * N_WEIGHT_LOADS)
            for n in range(2):
                dve.tensor_copy(wo_high[:, 4 * n:4 * n + 4, :], wo_sb[:, 4 * n:4 * n + 4, :]).then_inc(wo_split, 1)
            for n in range(2):
                dve.wait_ge(wo_split, n + 1)
                dve.tensor_tensor(wo_low[:, 4 * n:4 * n + 4, :], wo_sb[:, 4 * n:4 * n + 4, :], wo_high[:, 4 * n:4 * n + 4, :], ALU.subtract).then_inc(wo_split, 1)

            def tile_statistics(k, par):
                dve.wait_ge(fx_loaded[par].sem, fx_loaded[par].value(k // 2))
                ln_statistics(k, fx[:, par, :, 0:C], fstats, fmv, fln_step, TS)

            def tile_normalize(k, par):
                if begun(k - 1):
                    dve.wait_ge(fzT_made.sem, fzT_made.value(k - 1))
                    dve.wait_ge(zb_made.sem, zb_made.value(k - 1))
                ln_normalize(k, fx[:, par, :, 0:C], fz, fmv, fln_step, frstd, fln_rstd, TS)

            def split_w1(k, par):
                dve.wait_ge(w1_loaded[par].sem, w1_loaded[par].value(k // 2))
                for kc in range(KC):
                    dve.tensor_copy(w1_high[:, par, kc, :], w1_sb[:, par, kc, :]).then_inc(w1_high_made.sem, 1)

            def split_z(k, par):
                for kc in range(KC):
                    dve.wait_ge(fzT_copied.sem, fzT_copied.value(k, kc + 1))
                    dve.tensor_copy(fzT_high[:, kc, :], fzT[:, kc, :]).then_inc(z_high_made.sem, 1)
                for kc in range(KC):
                    dve.wait_ge(z_high_made.sem, z_high_made.value(k, kc + 1))
                    dve.tensor_tensor(fzT_low[:, kc, :], fzT[:, kc, :], fzT_high[:, kc, :], ALU.subtract).then_inc(z_low_made.sem, 1)

            def split_h(b):
                for m in range(MI):
                    dve.wait_ge(gelu_done.sem, gelu_done.value(b, m + 1))
                    dve.tensor_copy(hT_high[:, m, :], hT[:, m, :]).then_inc(h_high_made.sem, 1)
                    if m in H_LOW_DVE:
                        dve.wait_ge(h_high_made.sem, h_high_made.value(b, m + 1))
                        dve.tensor_tensor(hT_low[:, m, :], hT[:, m, :], hT_high[:, m, :], ALU.subtract).then_inc(h_low_dve.sem, 1)

            def add_z(b, par):
                dve.wait_ge(zb_made.sem, zb_made.value(b))
                if begun(b - 1):
                    dve.wait_ge(final_made.sem, final_made.value(b - 1))
                for half in range(2):
                    dve.wait_ge(ffn_made.sem, ffn_made.value(b, half + 1))
                    dve.tensor_tensor(ysum[:, 2 * half:2 * half + 2, :], psum[:, 4 + half, :].rearrange("p (j c) -> p j c", j=2), zb[:, par, 2 * half:2 * half + 2, :], ALU.add).then_inc(ysum_made.sem, 1)

            def out_statistics(b):
                for j in range(TS):
                    dve.wait_ge(ysum_made.sem, ysum_made.value(b, j // 2 + 1))
                    dve.bn_stats(ostats[:, j, :], ysum[:, j, :]).then_inc(oln_step.sem, 1)
                for j in range(TS):
                    dve.wait_ge(oln_step.sem, oln_step.value(b, j + 1))
                    dve.sem_inc(passed_dve, 1)
                    dve.bn_aggr(omv[:, j, :], ostats[:, j, :]).then_inc(oln_step.sem, 1)

            def finish(b, par):
                for j in range(TS):
                    dve.wait_ge(oln_step.sem, oln_step.value(b, TS + j + 1))
                    dve.scalar_tensor_tensor(ysum[:, j, :], ysum[:, j, :], omv[:, j, 0:1], gamma_sb[:], ALU.subtract, ALU.mult).then_inc(oln_step.sem, 1)
                dve.wait_ge(oln_rstd.sem, oln_rstd.value(b))
                dve.wait_ge(xb_made.sem, xb_made.value(b))
                if begun(b - 2):
                    dve.wait_ge(sent[par].sem, sent[par].value((b - 2) // 2))
                for j in range(TS):
                    dve.wait_ge(oln_step.sem, oln_step.value(b, 2 * TS + j + 1))
                    dve.scalar_tensor_tensor(final[:, par, j, :], ysum[:, j, :], orstd[:, j:j + 1], xb[:, par, j, :], ALU.mult, ALU.add).then_inc(final_made.sem, 1)
                dve.tensor_copy(number_u[:, par, :], number_f[:, par, :]).then_inc(numbers_made.sem, 1)

            def keep_numbers(k, par):
                dve.wait_ge(fx_loaded[par].sem, fx_loaded[par].value(k // 2))
                if begun(k - 2):
                    dve.wait_ge(numbers_made.sem, numbers_made.value(k - 2))
                dve.tensor_copy(number_f[:, par, :], fx[:, par, :, C]).then_inc(number_kept.sem, 1)

            def tile_body(k, par):
                if tile_runs(k, 2):
                    add_z(k - 2, par)
                if tile_runs(k, 0):
                    split_w1(k, par)
                if tile_runs(k, 1):
                    split_h(k - 1)
                if tile_runs(k, 0):
                    split_z(k, par)
                if tile_runs(k, 2):
                    out_statistics(k - 2)
                if tile_runs(k, -1):
                    tile_statistics(k + 1, 1 - par)
                if tile_runs(k, 2):
                    dve.wait_ge(number_kept.sem, number_kept.value(k - 2))
                    finish(k - 2, par)
                if tile_runs(k, 0):
                    keep_numbers(k, par)
                if tile_runs(k, -1):
                    tile_normalize(k + 1, 1 - par)

            tile_statistics(0, 0)
            tile_normalize(0, 0)
            tile_steps(dve, tile_body)

        @block.gpsimd
        def _(pool):
            def root(b, step, mean_var, rs, made, eps, NT=NT):
                pool.wait_ge(step.sem, step.value(b, 2 * NT))
                pool.sem_inc(passed_pool, 1)
                pool.tensor_scalar(rs[:], mean_var[:, :, 1], eps, None, ALU.add).then_inc(made.sem, 1)
                pool.wait_ge(made.sem, made.value(b, 1))
                pool.sem_inc(passed_pool, 1)
                pool.tensor_tensor(rs[:], rs[:], minus_half[:, 0:NT], ALU.pow).then_inc(made.sem, 1)

            def send_rows(i, par):
                b = i - 4
                pool.wait_ge(place_step.sem, place_step.value(b))
                pool.sem_inc(passed_pool, 1)
                pool.wait_ge(x2_made.sem, x2_made.value(b))
                pool.sem_inc(passed_pool, 1)
                pool.wait_ge(number_made.sem, number_made.value(b))
                pool.sem_inc(passed_pool, 1)
                for t in range(NT):
                    pool.indirect_dma_start(out=rows_dram, out_offset=bass.IndirectOffsetOnAxis(ap=row_u[:, par, t:t + 1], axis=0),
                                            in_=x2[:, par, t, :], in_offset=None).then_inc(rows_sent[par].sem, 16)

            def split_k(i, par):
                b, q = i - 1, 1 - par
                R = slice(0, KR)
                pool.wait_ge(ckv_copied.sem, ckv_copied.value(b, 1))
                pool.sem_inc(passed_pool, 1)
                chain = [
                    lambda: pool.tensor_copy(kc_h[R], kc32[R]),
                    lambda: pool.tensor_tensor(kc_r[R], kc32[R], kc_h[R], ALU.subtract),
                    lambda: pool.tensor_copy(kc_m[R], kc_r[R]),
                    lambda: pool.tensor_tensor(kc_r2[R], kc_r[R], kc_m[R], ALU.subtract),
                    lambda: pool.tensor_scalar(kc_a[R], kc_h[R], part_mask[R, 0:1], None, ALU.mult),
                    lambda: pool.tensor_scalar(kc_b[R], kc_m[R], part_mask[R, 1:2], None, ALU.mult),
                    lambda: pool.tensor_tensor(kc_a[R], kc_a[R], kc_b[R], ALU.add),
                    lambda: pool.tensor_scalar(kc_b[R], kc_r2[R], part_mask[R, 2:3], None, ALU.mult),
                    lambda: pool.tensor_tensor(KCx[R, q, 0:M], kc_a[R], kc_b[R], ALU.add),
                ]
                if begun(b - 2):
                    pool.wait_ge(cst_made.sem, cst_made.value(b - 2))
                    pool.sem_inc(passed_pool, 1)
                for k, op in enumerate(chain):
                    if k:
                        pool.wait_ge(kc_step.sem, kc_step.value(b, k))
                        pool.sem_inc(passed_pool, 1)
                    op().then_inc(kc_step.sem, 1)

            def body(i, par):
                if runs(i, 0):
                    pool.wait_ge(q_mid.sem, q_mid.value(i))
                    pool.sem_inc(passed_pool, 1)
                    pool.tensor_tensor(q_parts[:, 2, :], q_rest[:], q_parts[:, 1, :], ALU.subtract).then_inc(q_low.sem, 1)
                    pool.wait_ge(k_mid.sem, k_mid.value(i))
                    pool.sem_inc(passed_pool, 1)
                    pool.tensor_tensor(k_parts[:, 2, :], k_rest[:], k_parts[:, 1, :], ALU.subtract).then_inc(k_low.sem, 1)
                if runs(i, 2):
                    pool.wait_ge(cq_mid.sem, cq_mid.value(i - 2))
                    pool.sem_inc(passed_pool, 1)
                    pool.tensor_tensor(cq_parts[:, 2, :], cq_rest[:], cq_parts[:, 1, :], ALU.subtract).then_inc(cq_low.sem, 1)
                if runs(i, 3):
                    root(i - 3, ln3_step, rmv, rrstd, ln3_rstd, LN_EPS)
                if runs(i, 0):
                    root(i + 1, ln1_step, mv, rstd, ln1_rstd, LN_EPS)
                if runs(i, 4):
                    send_rows(i, par)
                if runs(i, 1):
                    root(i - 1, ln2_step, cmv, crstd, ln2_rstd, LN_EPS)
                    split_k(i, par)

            pool.wait_ge(consts_ready, VECTOR_CONSTS)
            root(0, ln1_step, mv, rstd, ln1_rstd, LN_EPS)
            pool.memset(V[:], 0.0).then_inc(gpsimd_consts, 1)
            pool.wait_ge(gpsimd_consts, 1)
            pool.memset(V[:, 0, :, :, D:D + 1], 1.0).then_inc(gpsimd_consts, 1)
            pool.wait_ge(gpsimd_consts, 2)
            pool.memset(V[:, 1, :, :, D:D + 1], 1.0).then_inc(gpsimd_consts, 1)
            pool.wait_ge(gpsimd_consts, 3)
            pool.memset(VC[:], 0.0).then_inc(gpsimd_consts, 1)
            pool.wait_ge(gpsimd_consts, 4)
            pool.memset(KCx[KR:P], 1.0).then_inc(gpsimd_consts, 1)
            pool.wait_ge(gpsimd_consts, 5)
            pool.memset(QC[KR:KR + 1], 1.0).then_inc(gpsimd_consts, 1)
            pool.wait_ge(gpsimd_consts, 6)
            pool.memset(KP[KR:P], 1.0).then_inc(gpsimd_consts, 1)
            pool.wait_ge(gpsimd_consts, GPSIMD_CONSTS)
            pool.wait_ge(weights_in, 16 * N_WEIGHT_LOADS)
            pool.memset(padding[:, :, 0:C], 0.0).then_inc(padding_made, 1)
            pool.memset(padding[:, :, C:ROW], float(B * T)).then_inc(padding_made, 1)
            steps(pool, body)

            pool.wait_ge(rank_made.sem, rank_made.value(B - 1))
            pool.wait_ge(rzT_copied.sem, rzT_copied.value(B - 1))
            pool.wait_ge(place_step.sem, place_step.value(B - 1))
            pool.wait_ge(kc_step.sem, kc_step.value(B - 1))
            pool.wait_ge(ln3_rstd.sem, ln3_rstd.value(B - 1))
            for par in range(2):
                pool.wait_ge(x_loaded[par].sem, x_loaded[par].value(B // 2))
                pool.wait_ge(rows_sent[par].sem, rows_sent[par].value(B // 2 - 1))

            def send_tile(b, par):
                pool.wait_ge(numbers_made.sem, numbers_made.value(b))
                pool.sem_inc(passed_pool, 1)
                for j in range(TS):
                    pool.wait_ge(final_made.sem, final_made.value(b, j + 1))
                    pool.sem_inc(passed_pool, 1)
                    pool.indirect_dma_start(out=out.rearrange("b t c -> (b t) c"), out_offset=bass.IndirectOffsetOnAxis(ap=number_u[:, par, j:j + 1], axis=0),
                                            in_=final[:, par, j, :], in_offset=None, bounds_check=B * T - 1, oob_is_err=False).then_inc(sent[par].sem, 16)

            def tile_body(k, par):
                if tile_runs(k, 0):
                    for kc in range(KC):
                        pool.wait_ge(w1_high_made.sem, w1_high_made.value(k, kc + 1))
                        pool.sem_inc(passed_pool, 1)
                        pool.tensor_tensor(w1_low[:, par, kc, :], w1_sb[:, par, kc, :], w1_high[:, par, kc, :], ALU.subtract).then_inc(w1_low_made.sem, 1)
                    if begun(k - 2):
                        pool.wait_ge(ysum_made.sem, ysum_made.value(k - 2))
                        pool.sem_inc(passed_pool, 1)
                    pool.wait_ge(fln_step.sem, fln_step.value(k))
                    pool.sem_inc(passed_pool, 1)
                    pool.tensor_tensor(zb[:, par], fz[:], bo_sb[:].unsqueeze(1).broadcast_to([P, TS, C]), ALU.add).then_inc(zb_made.sem, 1)
                if tile_runs(k, 1):
                    for m in H_LOW_POOL:
                        pool.wait_ge(h_high_made.sem, h_high_made.value(k - 1, m + 1))
                        pool.sem_inc(passed_pool, 1)
                        pool.tensor_tensor(hT_low[:, m, :], hT[:, m, :], hT_high[:, m, :], ALU.subtract).then_inc(h_low_pool.sem, 1)
                if tile_runs(k, 2):
                    root(k - 2, oln_step, omv, orstd, oln_rstd, OUT_LN_EPS, TS)
                if tile_runs(k, -1):
                    root(k + 1, fln_step, fmv, frstd, fln_rstd, LN_EPS, TS)
                if tile_runs(k, 0):
                    if begun(k - 2):
                        pool.wait_ge(final_made.sem, final_made.value(k - 2))
                        pool.sem_inc(passed_pool, 1)
                    pool.wait_ge(fx_loaded[par].sem, fx_loaded[par].value(k // 2))
                    pool.sem_inc(passed_pool, 1)
                    pool.tensor_tensor(xb[:, par], fx[:, par, :, 0:C], beta_sb[:].unsqueeze(1).broadcast_to([P, TS, C]), ALU.add).then_inc(xb_made.sem, 1)
                if tile_runs(k, 2):
                    send_tile(k - 2, par)

            root(0, fln_step, fmv, frstd, fln_rstd, LN_EPS, TS)
            tile_steps(pool, tile_body)
            for k in (TILES - 2, TILES - 1):
                pool.wait_ge(sent[k % 2].sem, sent[k % 2].value(k // 2))
                pool.sem_inc(passed_pool, 1)


def kernel(**inputs):
    import numpy as np
    import concourse.bacc as bacc
    from concourse.bass_utils import run_bass_kernel_spmd

    arrays = layout(inputs)
    nc = bacc.Bacc("TRN2", target_bir_lowering=False, num_devices=1)
    args = [nc.dram_tensor(f"in_{name}", a.shape, mybir.dt.from_np(a.dtype), kind="ExternalInput").ap() for name, a in arrays.items()]
    shape = inputs["x"].shape
    args.append(nc.dram_tensor("out_dram", shape, F32, kind="ExternalOutput").ap())
    decoder_kernel(nc, *args)
    result = run_bass_kernel_spmd(nc, [{f"in_{name}": a for name, a in arrays.items()}], core_ids=[0])
    return result.results[0]["out_dram"]


def layout(inputs):
    import numpy as np

    def c(a):
        return np.ascontiguousarray(a)

    i = {k: np.asarray(v) for k, v in inputs.items()}
    row, col = np.arange(P)[:, None], np.arange(P)[None, :]
    tiles = i["x"].shape[0] * T // TILE + E - 1
    consts = np.zeros((P, TILE_NOS + tiles), np.float32)
    consts[:, TILE_NOS:] = np.arange(tiles)
    consts[:, 0:P] = np.eye(P)
    consts[:, P:2 * P] = np.where(col > row, NEG, 0.0)
    consts[:, 2 * P:3 * P] = np.where(row > col, NEG, 0.0)
    consts[:, 3 * P:3 * P + M] = np.arange(M)
    for t, part in enumerate(K_PARTS):
        consts[D * t:D * t + D, 3 * P + M + part] = 1.0
    tokens = i["x"].shape[0] * T
    consts[:, BEFORE - E:BEFORE] = E - np.arange(E)
    consts[:, BEFORE:BEFORE + P] = row < col
    consts[:, NEXT_ROW:NEXT_ROW + E] = np.arange(E) * (tokens + TILE)
    consts[:, NUMBERS:TILE_NOS] = row + P * np.arange(2 * NT)[None, :] - 2 * T
    return {
        "x": c(i["x"]),
        "ctxT": c(i["ctx_1024"].transpose(0, 2, 1)),
        "wqkvT": c(i["L0_attn_W"].T),
        "bqkT": c(i["L0_attn_b"][:2 * C].reshape(2 * KC, P).T),
        "bv": c(i["L0_attn_b"][2 * C:].reshape(1, C)),
        "wqT": c(i["L0_xattn_Wq"].T),
        "wkvT": c(i["L0_xattn_Wkv"].T),
        "wcT": c(i["L0_xattn_Wc"].T),
        "w_router": c(i["L0_ffn_W_router"]),
        "w1": c(i["L0_ffn_W1"]),
        "b1T": c(i["L0_ffn_b1"].reshape(E, MI, P).transpose(0, 2, 1)),
        "wo": c(i["L0_ffn_Wo"]),
        "bo": c(i["L0_ffn_bo"].reshape(1, C)),
        "gamma": c(i["L0_ffn_ln_gamma"].reshape(1, C)),
        "beta": c(i["L0_ffn_ln_beta"].reshape(1, C)),
        "consts": consts,
    }
```
